# Optimizing a Trainium2 kernel written in Bass

```python
import numpy as np
import jax
import jax.numpy as jnp

def _softmax(x, axis=-1):
    return jax.nn.softmax(x, axis=axis)

def _gelu(x):
    return jax.nn.gelu(x, approximate=True)

def _silu(x):
    return jax.nn.silu(x)

def _sigmoid(x):
    return jax.nn.sigmoid(x)

def _layernorm(x, axis=-1, eps=1e-05):
    m = jnp.mean(x, axis=axis, keepdims=True)
    v = jnp.var(x, axis=axis, keepdims=True)
    return (x - m) / jnp.sqrt(v + eps)

def _scatter_add(tgt, idx, src, axis=0):
    return tgt.at[idx].add(src)

def _segment_sum(src, seg, n):
    return jax.ops.segment_sum(src, seg, n)
kernel_name = 'mk_adj_resnorm_d1_adj_r2_d3861d'

def setup_inputs(seed: int=0):
    np.random.seed(seed)
    _w = jnp.asarray

    def _rec_inputs():
        import jax
        import jax.numpy as jnp
        _gk = jax.random.key(seed)
        x = 7.22e-05 + 1 * jax.random.normal(jax.random.fold_in(_gk, 1), (32, 256, 128), jnp.float32)
        _w = (1.0 + jnp.arange(256, dtype=jnp.float32)) ** (-0.5)
        _w = _w / _w.mean()
        _pij = jnp.clip(0.015625 * _w[:, None] * _w[None, :], 0.0, 1.0)
        _a = jax.random.uniform(jax.random.fold_in(_gk, 2), (32, 256, 256)) < _pij
        _a = jnp.logical_or(_a, jnp.swapaxes(_a, -1, -2))
        _a = jnp.logical_or(_a, jnp.eye(256, dtype=bool))
        _af = _a.astype(jnp.float32)
        adj = _af
        return (x, adj)
    x, adj = _rec_inputs()

    def _L0_gnn_setup():
        import jax, jax.numpy as jnp
        import numpy as np
        from jax import lax
        DIM = 128
        EPS = 1e-05

        def _bn(h, g, b, m, v):
            scale = g / jnp.sqrt(v + EPS)
            return h * scale[None, :, None] + (b - m * scale)[None, :, None]

        def _conv1d(h, w, pad):
            return lax.conv_general_dilated(h, w, window_strides=(1,), padding=[(pad, pad)], dimension_numbers=('NCH', 'OIH', 'NCH'))
        key = jax.random.key(seed)
        ks = jax.random.split(key, 16)
        bs, n, d = (16, 1024, DIM)
        s = 0.05
        return {'x': jax.random.normal(ks[0], (bs, n, d), jnp.float32), 'mask': jnp.ones((bs, n, n), jnp.float32), 'w_se': jax.random.normal(ks[1], (3, d), jnp.float32) * s, 'b_se': jnp.zeros((3,), jnp.float32), 'conv1_w': jax.random.normal(ks[2], (d, d, 1), jnp.float32) * s, 'bn1_g': jnp.ones((d,), jnp.float32), 'bn1_b': jnp.zeros((d,), jnp.float32), 'bn1_m': jnp.zeros((d,), jnp.float32), 'bn1_v': jnp.ones((d,), jnp.float32), 'conv2_w': jax.random.normal(ks[3], (d, d, 17), jnp.float32) * s, 'bn2_g': jnp.ones((d,), jnp.float32), 'bn2_b': jnp.zeros((d,), jnp.float32), 'bn2_m': jnp.zeros((d,), jnp.float32), 'bn2_v': jnp.ones((d,), jnp.float32), 'w_msg': jax.random.normal(ks[4], (d, d), jnp.float32) * s, 'b_msg': jnp.zeros((d,), jnp.float32), 'w_ih': jax.random.normal(ks[5], (3 * d, 2 * d), jnp.float32) * s, 'b_ih': jnp.zeros((3 * d,), jnp.float32), 'w_hh': jax.random.normal(ks[6], (3 * d, d), jnp.float32) * s, 'b_hh': jnp.zeros((3 * d,), jnp.float32)}
    _L0_gnn_all = _L0_gnn_setup()
    _L0_gnn_in = {k: v for k, v in _L0_gnn_all.items() if k in ('w_se', 'b_se', 'conv1_w', 'bn1_g', 'bn1_b', 'bn1_m', 'bn1_v', 'conv2_w', 'bn2_g', 'bn2_b', 'bn2_m', 'bn2_v', 'w_msg', 'b_msg', 'w_ih', 'b_ih', 'w_hh', 'b_hh')}
    del _L0_gnn_all
    return {'x': x, 'adj': adj, 'L0_gnn_w_se': _L0_gnn_in['w_se'], 'L0_gnn_b_se': _L0_gnn_in['b_se'], 'L0_gnn_conv1_w': _L0_gnn_in['conv1_w'], 'L0_gnn_bn1_g': _L0_gnn_in['bn1_g'], 'L0_gnn_bn1_b': _L0_gnn_in['bn1_b'], 'L0_gnn_bn1_m': _L0_gnn_in['bn1_m'], 'L0_gnn_bn1_v': _L0_gnn_in['bn1_v'], 'L0_gnn_conv2_w': _L0_gnn_in['conv2_w'], 'L0_gnn_bn2_g': _L0_gnn_in['bn2_g'], 'L0_gnn_bn2_b': _L0_gnn_in['bn2_b'], 'L0_gnn_bn2_m': _L0_gnn_in['bn2_m'], 'L0_gnn_bn2_v': _L0_gnn_in['bn2_v'], 'L0_gnn_w_msg': _L0_gnn_in['w_msg'], 'L0_gnn_b_msg': _L0_gnn_in['b_msg'], 'L0_gnn_w_ih': _L0_gnn_in['w_ih'], 'L0_gnn_b_ih': _L0_gnn_in['b_ih'], 'L0_gnn_w_hh': _L0_gnn_in['w_hh'], 'L0_gnn_b_hh': _L0_gnn_in['b_hh']}

def reference(x, adj, L0_gnn_w_se, L0_gnn_b_se, L0_gnn_conv1_w, L0_gnn_bn1_g, L0_gnn_bn1_b, L0_gnn_bn1_m, L0_gnn_bn1_v, L0_gnn_conv2_w, L0_gnn_bn2_g, L0_gnn_bn2_b, L0_gnn_bn2_m, L0_gnn_bn2_v, L0_gnn_w_msg, L0_gnn_b_msg, L0_gnn_w_ih, L0_gnn_b_ih, L0_gnn_w_hh, L0_gnn_b_hh):
    import jax
    import jax.numpy as jnp

    def _L0_gnn_ref(x, mask, w_se, b_se, conv1_w, bn1_g, bn1_b, bn1_m, bn1_v, conv2_w, bn2_g, bn2_b, bn2_m, bn2_v, w_msg, b_msg, w_ih, b_ih, w_hh, b_hh):
        import jax, jax.numpy as jnp
        import numpy as np
        from jax import lax
        DIM = 128
        EPS = 1e-05

        def _bn(h, g, b, m, v):
            scale = g / jnp.sqrt(v + EPS)
            return h * scale[None, :, None] + (b - m * scale)[None, :, None]

        def _conv1d(h, w, pad):
            return lax.conv_general_dilated(h, w, window_strides=(1,), padding=[(pad, pad)], dimension_numbers=('NCH', 'OIH', 'NCH'))
        d = x.shape[-1]
        xc = jnp.transpose(x, (0, 2, 1))
        h = _bn(_conv1d(xc, conv1_w, 0), bn1_g, bn1_b, bn1_m, bn1_v)
        h = jax.nn.relu(h)
        h = _bn(_conv1d(h, conv2_w, 8), bn2_g, bn2_b, bn2_m, bn2_v)
        x_conv = jnp.transpose(jax.nn.relu(h + xc), (0, 2, 1))
        s = x @ w_se.T + b_se
        sq = jnp.sum(s * s, axis=-1)
        dist = sq[:, :, None] + sq[:, None, :] - 2.0 * jnp.einsum('bnd,bmd->bnm', s, s)
        A = jnp.exp(-dist) * mask
        msg = jax.nn.relu(x @ w_msg.T + b_msg)
        x_nmp = jnp.einsum('bnm,bmd->bnd', A, msg)
        x_in = jnp.concatenate([x_conv, x_nmp], axis=-1)
        gi = x_in @ w_ih.T + b_ih
        gh = x @ w_hh.T + b_hh
        gi_r, gi_z, gi_n = (gi[..., :d], gi[..., d:2 * d], gi[..., 2 * d:])
        gh_r, gh_z, gh_n = (gh[..., :d], gh[..., d:2 * d], gh[..., 2 * d:])
        r = jax.nn.sigmoid(gi_r + gh_r)
        z = jax.nn.sigmoid(gi_z + gh_z)
        nn_ = jnp.tanh(gi_n + r * gh_n)
        return (1.0 - z) * nn_ + z * x
    x = _layernorm(x + _L0_gnn_ref(x, adj, L0_gnn_w_se, L0_gnn_b_se, L0_gnn_conv1_w, L0_gnn_bn1_g, L0_gnn_bn1_b, L0_gnn_bn1_m, L0_gnn_bn1_v, L0_gnn_conv2_w, L0_gnn_bn2_g, L0_gnn_bn2_b, L0_gnn_bn2_m, L0_gnn_bn2_v, L0_gnn_w_msg, L0_gnn_b_msg, L0_gnn_w_ih, L0_gnn_b_ih, L0_gnn_w_hh, L0_gnn_b_hh), axis=-1)
    return x

_drawn_inputs = setup_inputs


def setup_inputs(seed=0):
    import zlib

    import numpy as np

    out = dict(_drawn_inputs(seed))
    spreads = {'L0_gnn_b_se': (0.0, 2.0),
     'L0_gnn_bn1_g': (1.0, 0.6),
     'L0_gnn_bn1_b': (0.0, 0.462),
     'L0_gnn_bn1_m': (0.0, 0.418),
     'L0_gnn_bn1_v': (1.0, 0.6),
     'L0_gnn_bn2_g': (1.0, 0.6),
     'L0_gnn_bn2_b': (0.0, 0.7),
     'L0_gnn_bn2_m': (0.0, 0.644),
     'L0_gnn_bn2_v': (1.0, 0.6),
     'L0_gnn_b_msg': (0.0, 0.278),
     'L0_gnn_b_ih': (0.0, 0.295),
     'L0_gnn_b_hh': (0.0, 0.371)}
    factors = {}
    for name, (base, spread) in spreads.items():
        noise = np.random.default_rng([zlib.crc32(name.encode()), seed]).standard_normal(out[name].shape)
        drawn = base * np.exp(spread * noise) if base else spread * noise
        out[name] = jnp.asarray(drawn.astype(out[name].dtype))
    for name, factor in factors.items():
        out[name] = (out[name] * factor).astype(out[name].dtype)
    return out
```

```python
from contextlib import ExitStack

import numpy as np

import concourse.bass as bass
from concourse import mybir

ALU = mybir.AluOpType
ACT = mybir.ActivationFunctionType
F32 = mybir.dt.float32
F32R = mybir.dt.float32r

P = 128
B = 32
N = 256
TAPS = 17
PAD = 8
EPS = 1e-5
GB = 8
NG = B // GB
C = GB * N
PH = 4
NI = N // PH
J = (N + 2 * PAD) // PH
JP = PAD // PH
CH = 512
NC = C // CH
MB = N // P
TG = TAPS // 4
SL = GB * J
QS = SL // 2
STACK = 20

F0, F1, F2, F3, D2, D3, E1, E3, H3 = range(9)
NS = 9
S01, S02, S13, S23, S0123 = range(4, 9)
PRODUCTS = [
    (H3, S0123, True), (D2, S02, True), (D3, S13, False),
    (E1, S01, True), (F0, 0, True), (F1, 1, False),
    (E3, S23, False), (F2, 2, False), (F3, 3, False),
]
(G1, B1, M1, V1, G2, B2, M2, V2, BIR, BIZ, BIN, BHR, BHZ, BHN) = range(14)
NPAR = 14
(KAL, KCL, KAR, KCR, KNL, KNR, KNM) = range(7)
NCON = 7
(SC1, SH1, SC2, SH2, BR, BZ, BN, BH, BSE, BL, BRR, TMP, TMQ, ISD1, ISD2) = range(15)
NVEC = 15
(HHR, HHZ, HHN, ICR, ICZ, ICN, IMR, IMZ, IMN, W1, WMSG) = range(11)
NW = 11
ZW = 224


def build(nc, xt_d, xn_d, adj_d, wsm_d, wse_d, wcv_d, bn2_d, par_d, bmsg_d, bse_d,
          con_d, sel_d, selb_d, idn_d, out_d):
    with ExitStack() as ctx:
        def sb(name, shape, dt=F32):
            return ctx.enter_context(nc.sbuf_tensor(name, shape, dt))

        def sem(name):
            return ctx.enter_context(nc.semaphore(name))

        x = sb("x", [P, C])
        x_hi, x_lo = sb("x_hi", [P, C], F32R), sb("x_lo", [P, C], F32R)
        xn = sb("xn", [P, C // P, P])
        adj = sb("adj", [P, 2, 2, MB, N])
        H = sb("H", [P, PH, SL])
        EF = sb("EF", [P, 10, QS])
        V_hi, V_lo = sb("V_hi", [P, NS, SL], F32R), sb("V_lo", [P, NS, SL], F32R)
        cw_hi = sb("cw_hi", [P, TAPS + 5 * TG, P], F32R)
        cw_lo = sb("cw_lo", [P, TAPS + 5 * TG, P], F32R)
        w_hi, w_lo = sb("w_hi", [P, NW, P], F32R), sb("w_lo", [P, NW, P], F32R)
        z_hi, z_lo = sb("z_hi", [P, ZW], F32R), sb("z_lo", [P, ZW], F32R)
        sel = sb("sel", [P, P])
        idn = sb("idn", [P, P])
        selb = sb("selb", [3, P])
        bse = sb("bse", [3, 1])
        bmsg = sb("bmsg", [2, P])
        bmsg_r = sb("bmsg_r", [2, P], F32R)
        ones_r = sb("ones_r", [2, P], F32R)
        par = sb("par", [P, NPAR])
        con = sb("con", [P, NCON])
        vec = sb("vec", [P, NVEC])
        L, R = sb("L", [P, 2, N], F32R), sb("R", [P, 2, N], F32R)
        msg = sb("msg", [P, 2, MB, P])
        m_hi, m_lo = sb("m_hi", [P, C], F32R), sb("m_lo", [P, C], F32R)
        c_hi, c_lo = sb("c_hi", [P, C], F32R), sb("c_lo", [P, C], F32R)
        r, z, hn = sb("r", [P, 2, CH]), sb("z", [P, 2, CH]), sb("hn", [P, 2, CH])
        stats = sb("stats", [P, NC, 6])
        mv = sb("mv", [P, NC, 2])
        rstd = sb("rstd", [P, NC])
        pconst = sb("pconst", [P, 3])

        A = r
        VL, VR = z, hn
        P1 = EF[:, :, :].rearrange("p a b -> p (a b)")[:, 0:2 * CH].rearrange("p (c n) -> p c n", c=2)
        S = EF[:, :, :].rearrange("p a b -> p (a b)")[:, 2 * CH:4 * CH].rearrange("p (c n) -> p c n", c=2)
        wraw = EF[:, :, :].rearrange("p a b -> p (a b)")[:, 0:NW * P + 3]
        cwsum = EF[:, :, :].rearrange("p a b -> p (a b)")[:, 0:5 * TG * P].rearrange(
            "p (g s o) -> p g s o", g=TG, s=5)
        cwraw = H[:, :, :].rearrange("p a b -> p (a b)").rearrange("p (t o) -> p t o", t=TAPS)
        bn2row = xn[:, 0:4, :]

        bank = [ctx.enter_context(nc.psum_tensor(f"bank{i}", [P, CH], F32)) for i in range(8)]
        conv1_bank = [bank[0], bank[1]]
        nmp_bank = [bank[0], bank[1]]
        u_bank = [bank[2], bank[7]]
        dist_bank = [bank[3], bank[4]]
        msg_bank = [bank[5], bank[6]]
        conv2_bank = [bank[6], bank[7], bank[0], bank[1]]
        r_bank, z_bank, in_bank, hn_bank = bank[2], bank[3], bank[4], bank[5]
        turn_bank = [bank[6], bank[7]]

        x_loaded = [sem(f"x_loaded{k}") for k in range(NC)]
        xn_loaded = [sem(f"xn_loaded{k}") for k in range(NC)]
        adj_loaded = [sem(f"adj_loaded{s}") for s in range(2)]
        out_stored = [sem(f"out_stored{k}") for k in range(NC)]
        small_loaded, cw_loaded, par_loaded = sem("small_loaded"), sem("cw_loaded"), sem("par_loaded")
        bse_spread, setup_step = sem("bse_spread"), sem("setup_step")
        small_ready, vec_ready, cw_ready = sem("small_ready"), sem("vec_ready"), sem("cw_ready")
        bn_rsqrt_ready = sem("bn_rsqrt_ready")
        pconst_ready, eps_added = sem("pconst_ready"), sem("eps_added")
        pads_zero = sem("pads_zero")
        xhi_ready, x_ready = sem("xhi_ready"), sem("x_ready")
        conv1_done, h_ready = sem("conv1_done"), sem("h_ready")
        u_done, sq_ready, usum_done = sem("u_done"), sem("sq_ready"), sem("usum_done")
        lrhi_ready, lr_ready = sem("lrhi_ready"), sem("lr_ready")
        msg_done, msg_ready = sem("msg_done"), sem("msg_ready")
        dist_done, exp_ready, a_ready = sem("dist_done"), sem("exp_ready"), sem("a_ready")
        nmp_done, mhi_ready, m_ready = sem("nmp_done"), sem("mhi_ready"), sem("m_ready")
        e_ready, ef_ready, vhi_ready, v_ready = sem("e_ready"), sem("ef_ready"), sem("vhi_ready"), sem("v_ready")
        conv2_done, s_ready, prod_used = sem("conv2_done"), sem("s_ready"), sem("prod_used")
        p_ready, t_ready, chi_ready, c_ready = sem("p_ready"), sem("t_ready"), sem("chi_ready"), sem("c_ready")
        t_step = sem("t_step")
        rhn_done, zin_done = sem("rhn_done"), sem("zin_done")
        r_ready, hn_ready, z_ready, n_ready = sem("r_ready"), sem("hn_ready"), sem("z_ready"), sem("n_ready")
        gated_ready, narg_ready, e_gru_ready, f_ready = (
            sem("gated_ready"), sem("narg_ready"), sem("e_gru_ready"), sem("f_ready"))
        turn_done, y_ready = sem("turn_done"), sem("y_ready")
        stats_ready, mv_ready, rstd_ready, out_ready = (
            sem("stats_ready"), sem("mv_ready"), sem("rstd_ready"), sem("out_ready"))

        block = ctx.enter_context(nc.Block())

        def chunk(t, k):
            return t[:, k * CH:(k + 1) * CH]

        def nodes(t, b, mb):
            return t[:, b * N + mb * P:b * N + (mb + 1) * P]

        def half(t, s, q):
            return t[:, s, q * QS:(q + 1) * QS]

        def phases(t):
            return t[:, :].rearrange("p (b c i) -> p c b i", b=GB, c=PH)

        def inner(c0, c1):
            return H[:, c0:c1, :].rearrange("p c (b j) -> p c b j", b=GB)[:, :, :, JP:JP + NI]

        def f32(ap):
            return ap.bitcast(F32)

        @block.sync
        def _(sp):
            def load_x(g, k):
                sp.dma_start(chunk(x, k), xt_d[g, :, k * CH:(k + 1) * CH]).then_inc(x_loaded[k], 16)

            def load_xn(g, k):
                sp.dma_start(xn[:, 4 * k:4 * k + 4, :], xn_d[g, :, 4 * k:4 * k + 4, :]).then_inc(xn_loaded[k], 16)

            def load_adj(g, pair):
                sp.dma_start(adj[:, pair % 2], adj_d[g, pair]).then_inc(adj_loaded[pair % 2], 16)

            def store(g, k):
                sp.wait_ge(out_ready, 4 * g + k + 1)
                sp.dma_start(out_d[g, :, 4 * k:4 * k + 4, :], xn[:, 4 * k:4 * k + 4, :]).then_inc(out_stored[k], 16)

            def body(g, last):
                for pair in range(2, 4):
                    sp.wait_ge(a_ready, 8 * g + 2 * pair - 2)
                    load_adj(g, pair)
                if not last:
                    for pair in range(2):
                        sp.wait_ge(a_ready, 8 * g + 2 * pair + 6)
                        load_adj(g + 1, pair)
                for k in range(NC + 1):
                    if not last and k < NC:
                        sp.wait_ge(e_gru_ready, 4 * g + k + 1)
                        load_x(g + 1, k)
                    if k >= 1:
                        store(g, k - 1)
                if not last:
                    for k in range(NC):
                        sp.wait_ge(out_stored[k], 16 * g + 16)
                        load_xn(g + 1, k)

            for k in range(NC):
                load_x(0, k)
                if k == 0:
                    sp.dma_start(par[:, :], par_d[:, :]).then_inc(par_loaded, 16)
                    sp.dma_start(con[:, :], con_d[:, :]).then_inc(par_loaded, 16)
                    sp.dma_start(selb[:, :], selb_d[:, :]).then_inc(par_loaded, 16)
                    sp.dma_start(bse[:, :], bse_d[:, :]).then_inc(par_loaded, 16)
                    sp.dma_start(bn2row[:, 0:2, :], bn2_d[:, :].partition_broadcast(P)).then_inc(par_loaded, 16)
                    sp.dma_start(wraw[:, 0:NW * P], wsm_d[:, :]).then_inc(small_loaded, 16)
                    sp.dma_start(wraw[:, NW * P:NW * P + 3], wse_d[:, :]).then_inc(small_loaded, 16)
                    sp.dma_start(bmsg[:, :], bmsg_d[:, :]).then_inc(small_loaded, 16)
                    sp.dma_start(sel[:, :], sel_d[:, :]).then_inc(small_loaded, 16)
                    sp.dma_start(idn[:, :], idn_d[:, :]).then_inc(small_loaded, 16)
            sp.dma_start(cwraw, wcv_d[:, :, :]).then_inc(cw_loaded, 16)
            load_adj(0, 0)
            load_adj(0, 1)
            sp.wait_ge(cw_ready, 1)
            for k in range(NC):
                load_xn(0, k)
            with sp.Fori(0, NG - 1) as g:
                body(g, False)
            body(NG - 1, True)
            for k in range(NC):
                sp.wait_ge(out_stored[k], 16 * NG)

        @block.tensor
        def _(pe):
            def three(out, w_h, w_l, v_h, v_l, start, stop):
                nc.tensor.matmul(out, w_h, v_h, start=start, stop=False, skip_group_check=True)
                nc.tensor.matmul(out, w_h, v_l, start=False, stop=False, skip_group_check=True)
                return nc.tensor.matmul(out, w_l, v_h, start=False, stop=stop, skip_group_check=True)

            def conv1(g, k):
                pe.wait_ge(x_ready, 4 * g + k + 1)
                if k >= 2:
                    pe.wait_ge(h_ready, 4 * g + k - 1)
                three(conv1_bank[k % 2][:, :], w_hi[:, W1, :], w_lo[:, W1, :], chunk(x_hi, k), chunk(x_lo, k),
                      True, True).then_inc(conv1_done, 1)

            def u_rows(g, q):
                pe.wait_ge(x_ready, 4 * g + 2 * q + 2)
                for i in range(4):
                    b = 4 * q + i
                    s = slice(96 - 32 * i, ZW - 32 * i)
                    last = three(u_bank[q][:, 0:N], z_hi[:, s], z_lo[:, s], x_hi[:, b * N:(b + 1) * N],
                                 x_lo[:, b * N:(b + 1) * N], i == 0, False)
                last.then_inc(u_done, 1)

            def u_squares(g, q):
                pe.wait_ge(sq_ready, 2 * g + q + 1)
                nc.tensor.matmul(u_bank[q][:, 0:N], sel[:, :], VL[:, q, 0:N], start=False, stop=True,
                                 skip_group_check=True).then_inc(usum_done, 1)

            def messages(g, b):
                if b >= 2:
                    pe.wait_ge(msg_ready, 8 * g + b - 1)
                pe.wait_ge(x_ready, 4 * g + b // 2 + 1)
                out = msg_bank[b % 2]
                rows = bmsg_r[:, :].rearrange("p (o d) -> p o d", o=1).broadcast_to([2, MB, P])
                nc.tensor.matmul(out[:, 0:MB * P], ones_r[:, :], rows, start=True, stop=False, skip_group_check=True)
                for mb in range(MB):
                    cols = out[:, mb * P:(mb + 1) * P]
                    nc.tensor.matmul(cols, nodes(x_hi, b, mb), w_hi[:, WMSG, :], start=False, stop=False,
                                     skip_group_check=True)
                    nc.tensor.matmul(cols, nodes(x_hi, b, mb), w_lo[:, WMSG, :], start=False, stop=False,
                                     skip_group_check=True)
                    last = nc.tensor.matmul(cols, nodes(x_lo, b, mb), w_hi[:, WMSG, :], start=False,
                                            stop=(mb == MB - 1), skip_group_check=True)
                last.then_inc(msg_done, 1)

            def distances(g, b):
                q, i = b // 4, b % 4
                pe.wait_ge(lr_ready, 2 * g + q + 1)
                if b >= 2:
                    pe.wait_ge(exp_ready, 8 * g + b - 1)
                rows = slice(32 * i, 32 * i + STACK)
                for mb in range(MB):
                    last = nc.tensor.matmul(dist_bank[b % 2][:, mb * N:(mb + 1) * N], L[rows, q, mb * P:(mb + 1) * P],
                                            R[rows, q, :], start=True, stop=True, skip_group_check=True)
                last.then_inc(dist_done, 1)

            def gather(g, b):
                pair = b // 2
                pe.wait_ge(msg_ready, 8 * g + b + 1)
                pe.wait_ge(a_ready, 8 * g + b + 1)
                if b % 2 == 0:
                    if pair < 2:
                        pe.wait_ge(h_ready, 4 * g + pair + 3)
                    else:
                        pe.wait_ge(m_ready, 4 * g + pair - 1)
                for mb in range(MB):
                    last = nc.tensor.matmul(nmp_bank[pair % 2][:, (b % 2) * N:(b % 2 + 1) * N], msg[:, b % 2, mb, :],
                                            A[:, b % 2, mb * N:(mb + 1) * N], start=(mb == 0), stop=(mb == MB - 1),
                                            skip_group_check=True)
                last.then_inc(nmp_done, 1)

            def conv2(g):
                pe.wait_ge(v_ready, 2 * g + 2)
                for n, (slot, f, extra) in enumerate(PRODUCTS):
                    if n in (2, 3):
                        pe.wait_ge(m_ready, 4 * g + n + 1)
                    if n >= 4:
                        if (n - 4) % 3 == 0:
                            pe.wait_ge(s_ready, 3 * g + (n - 4) // 3 + 1)
                        else:
                            pe.wait_ge(prod_used, 6 * g + (n - 4) - (n - 4) // 3)
                    out = conv2_bank[n % 4][:, :]
                    for t in range(TG + extra):
                        w = 4 * t if t == TG else (4 * t + f if f < 4 else TAPS + 5 * t + f - 4)
                        vh = V_hi[:, slot, :].rearrange("p (b j) -> p b j", b=GB)[:, :, t:t + NI]
                        vl = V_lo[:, slot, :].rearrange("p (b j) -> p b j", b=GB)[:, :, t:t + NI]
                        last = three(out, cw_hi[:, w, :], cw_lo[:, w, :], vh, vl, t == 0, t == TG + extra - 1)
                    last.then_inc(conv2_done, 1)

            def gates(g, k):
                xs, ms, cs = ((chunk(a, k), chunk(b, k)) for a, b in ((x_hi, x_lo), (m_hi, m_lo), (c_hi, c_lo)))

                def part(out, w, v, start=False, stop=False):
                    return three(out[:, :], w_hi[:, w, :], w_lo[:, w, :], v[0], v[1], start, stop)
                if k == 0:
                    pe.wait_ge(m_ready, 4 * g + 4)
                if k >= 1:
                    pe.wait_ge(r_ready, 4 * g + k)
                part(r_bank, HHR, xs, start=True)
                part(r_bank, IMR, ms)
                if k >= 1:
                    pe.wait_ge(hn_ready, 4 * g + k)
                hn_last = part(hn_bank, HHN, xs, start=True, stop=True)
                if k >= 1:
                    part(r_bank, ICR, cs, stop=True).then_inc(rhn_done, 1)
                    pe.wait_ge(narg_ready, 4 * g + k)
                part(in_bank, IMN, ms, start=True)
                if k >= 1:
                    pe.wait_ge(z_ready, 4 * g + k)
                part(z_bank, HHZ, xs, start=True)
                part(z_bank, IMZ, ms)
                if k == 0:
                    pe.wait_ge(c_ready, 4 * g + 4)
                    part(r_bank, ICR, cs, stop=True).then_inc(rhn_done, 1)
                part(in_bank, ICN, cs, stop=True)
                part(z_bank, ICZ, cs, stop=True).then_inc(zin_done, 1)

            def turn(g, k):
                pe.wait_ge(f_ready, 4 * g + k + 1)
                if k >= 2:
                    pe.wait_ge(y_ready, 4 * g + k - 1)
                for j in range(NC):
                    last = nc.tensor.transpose(turn_bank[k % 2][:, j * P:(j + 1) * P],
                                               r[:, k % 2, j * P:(j + 1) * P], idn[:, :])
                last.then_inc(turn_done, 1)

            def body(g, last):
                u_rows(g, 0)
                messages(g, 0)
                u_squares(g, 0)
                messages(g, 1)
                distances(g, 0)
                distances(g, 1)
                conv1(g, 3)
                for b in range(GB):
                    gather(g, b)
                    if b == 0:
                        u_rows(g, 1)
                    if b == 1:
                        u_squares(g, 1)
                    if b + 2 < GB:
                        messages(g, b + 2)
                        distances(g, b + 2)
                conv2(g)
                for k in range(NC):
                    gates(g, k)
                    if not last and k >= 2:
                        conv1(g + 1, k - 2)
                    if k >= 1:
                        turn(g, k - 1)
                if not last:
                    conv1(g + 1, 2)
                turn(g, NC - 1)

            pe.wait_ge(par_loaded, 80)
            nc.tensor.matmul(bank[2][:, 0:1], selb[:, :], bse[:, :], start=True, stop=True).then_inc(bse_spread, 1)
            pe.wait_ge(small_ready, 1)
            pe.wait_ge(vec_ready, 1)
            pe.wait_ge(cw_ready, 1)
            for k in range(NC - 1):
                conv1(0, k)
            with pe.Fori(0, NG - 1) as g:
                body(g, False)
            body(NG - 1, True)

        @block.scalar
        def _(act):
            def v(c):
                return vec[:, c:c + 1]

            def split_x(g, k):
                act.wait_ge(x_loaded[k], 16 * g + 16)
                nc.scalar.activation(chunk(x_hi, k), chunk(x, k), ACT.Copy).then_inc(xhi_ready, 1)

            def relu1(g, k):
                act.wait_ge(conv1_done, 4 * g + k + 1)
                src = conv1_bank[k % 2][:, :].rearrange("p (b c i) -> p b c i", b=2, c=PH)
                dst = inner(0, PH)[:, :, 2 * k:2 * k + 2, :].rearrange("p c b i -> p b c i")
                nc.scalar.activation(dst, src, ACT.Relu, bias=v(SH1), scale=v(SC1)).then_inc(h_ready, 1)

            def squares(g, q):
                act.wait_ge(u_done, 2 * g + q + 1)
                nc.scalar.activation(VL[:, q, 0:N], u_bank[q][:, 0:N], ACT.Square, bias=v(BSE)).then_inc(sq_ready, 1)

            def operands(g, q):
                act.wait_ge(usum_done, 2 * g + q + 1)
                u = u_bank[q][:, 0:N]
                nc.scalar.activation(VL[:, q, 0:N], u, ACT.Identity, bias=v(BL), scale=con[:, KAL:KAL + 1])
                nc.scalar.activation(VR[:, q, 0:N], u, ACT.Identity, bias=v(BRR), scale=con[:, KAR:KAR + 1])
                nc.scalar.activation(L[:, q, :], u, ACT.Identity, bias=v(BL), scale=con[:, KAL:KAL + 1])
                nc.scalar.activation(R[:, q, :], u, ACT.Identity, bias=v(BRR),
                                     scale=con[:, KAR:KAR + 1]).then_inc(lrhi_ready, 1)

            def message(g, b):
                act.wait_ge(msg_done, 8 * g + b + 1)
                if b >= 2:
                    act.wait_ge(nmp_done, 8 * g + b - 1)
                nc.scalar.activation(msg[:, b % 2], msg_bank[b % 2][:, 0:MB * P].rearrange("p (m d) -> p m d", m=MB),
                                     ACT.Relu).then_inc(msg_ready, 1)

            def weights(g, b):
                act.wait_ge(dist_done, 8 * g + b + 1)
                nc.scalar.activation(A[:, b % 2, :], dist_bank[b % 2][:, :], ACT.Exp).then_inc(exp_ready, 1)

            def sums_hi(g, pair):
                act.wait_ge(nmp_done, 8 * g + 2 * pair + 2)
                nc.scalar.activation(chunk(m_hi, pair), nmp_bank[pair % 2][:, :], ACT.Copy).then_inc(mhi_ready, 1)

            def transformed_hi(g, q):
                act.wait_ge(ef_ready, 2 * g + q + 1)
                nc.scalar.activation(V_hi[:, F0:D3 + 1, q * QS:(q + 1) * QS], EF[:, 4:10, :], ACT.Copy)
                nc.scalar.activation(V_hi[:, E1:E3 + 1, q * QS:(q + 1) * QS],
                                     EF[:, 0:4, :].rearrange("p (a two) j -> p a two j", two=2)[:, :, 1, :], ACT.Copy)
                nc.scalar.activation(half(V_hi, H3, q), half(H, 3, q), ACT.Copy).then_inc(vhi_ready, 1)

            def shared(g, j):
                act.wait_ge(conv2_done, 9 * g + 3 * j + 1)
                if j == 2:
                    act.wait_ge(prod_used, 6 * g + 2)
                nc.scalar.activation(S[:, j % 2, :], conv2_bank[(3 * j) % 4][:, :], ACT.Identity,
                                     bias=(v(SH2) if j == 0 else 0.0)).then_inc(s_ready, 1)

            def relu2(g, h):
                act.wait_ge(t_ready, 2 * g + h + 1)
                for c in (2 * h, 2 * h + 1):
                    last = nc.scalar.activation(phases(c_hi)[:, c], inner(c, c + 1)[:, 0], ACT.Relu)
                    last.then_inc(chi_ready, 1)

            def body(g, last):
                squares(g, 0)
                message(g, 0)
                operands(g, 0)
                message(g, 1)
                weights(g, 0)
                weights(g, 1)
                split_x(g, 3)
                transformed_hi(g, 0)
                relu1(g, 3)
                for b in range(2, GB):
                    if b == 2:
                        squares(g, 1)
                    if b == 4:
                        operands(g, 1)
                    message(g, b)
                    weights(g, b)
                    if b % 2 == 0:
                        sums_hi(g, b // 2 - 1)
                    if b == 5:
                        transformed_hi(g, 1)
                sums_hi(g, 3)
                shared(g, 0)
                shared(g, 1)
                shared(g, 2)
                relu2(g, 0)
                relu2(g, 1)
                for k in range(NC):
                    act.wait_ge(rhn_done, 4 * g + k + 1)
                    nc.scalar.activation(r[:, k % 2, :], r_bank[:, :], ACT.Tanh, bias=v(BR), scale=0.5).then_inc(r_ready, 1)
                    nc.scalar.activation(hn[:, k % 2, :], hn_bank[:, :], ACT.Identity, bias=v(BH),
                                         scale=0.5).then_inc(hn_ready, 1)
                    act.wait_ge(zin_done, 4 * g + k + 1)
                    nc.scalar.activation(z[:, k % 2, :], z_bank[:, :], ACT.Tanh, bias=v(BZ), scale=0.5).then_inc(z_ready, 1)
                    if not last and k >= 1:
                        split_x(g + 1, k - 1)
                    act.wait_ge(narg_ready, 4 * g + k + 1)
                    nc.scalar.activation(hn[:, k % 2, :], hn[:, k % 2, :], ACT.Tanh, bias=v(BN)).then_inc(n_ready, 1)
                    if not last and k >= 2:
                        relu1(g + 1, k - 2)
                if not last:
                    relu1(g + 1, 2)

            act.wait_ge(vec_ready, 1)
            act.wait_ge(pads_zero, 1)
            for k in range(NC - 1):
                split_x(0, k)
            for k in range(NC - 1):
                relu1(0, k)
            with act.Fori(0, NG - 1) as g:
                body(g, False)
            body(NG - 1, True)

        @block.gpsimd
        def _(pool):
            def rsqrt(dst, src, eps, done, n):
                shape = [P, dst.shape[1]]
                nc.gpsimd.tensor_tensor(dst, src, eps.broadcast_to(shape), ALU.add).then_inc(eps_added, 1)
                pool.wait_ge(eps_added, n)
                nc.gpsimd.tensor_tensor(dst, dst, pconst[:, 2:3].broadcast_to(shape), ALU.pow).then_inc(done, 1)

            for c, value in enumerate((EPS, 4.0 * EPS, -0.5)):
                nc.gpsimd.memset(pconst[:, c:c + 1], value).then_inc(pconst_ready, 1)
            pool.wait_ge(pconst_ready, 3)
            pool.wait_ge(par_loaded, 80)
            rsqrt(vec[:, ISD1:ISD1 + 1], par[:, V1:V1 + 1], pconst[:, 0:1], bn_rsqrt_ready, 1)
            rsqrt(vec[:, ISD2:ISD2 + 1], par[:, V2:V2 + 1], pconst[:, 0:1], bn_rsqrt_ready, 2)
            rsqrt(bn2row[:, 2, :], bn2row[:, 1, :], pconst[:, 0:1], bn_rsqrt_ready, 3)
            with pool.Fori(0, NG) as g:
                for k in range(NC):
                    pool.wait_ge(mv_ready, 4 * g + k + 1)
                    rsqrt(rstd[:, :], mv[:, :, 1], pconst[:, 1:2], rstd_ready, 4 * g + k + 4)

        @block.vector
        def _(dve):
            steps = [0]

            def step(ins):
                steps[0] += 1
                ins.then_inc(setup_step, 1)
                dve.wait_ge(setup_step, steps[0])

            def v(c):
                return vec[:, c:c + 1]

            def p(c):
                return par[:, c:c + 1]

            TT, TS, STT = nc.vector.tensor_tensor, nc.vector.tensor_scalar, nc.vector.scalar_tensor_tensor

            def setup():
                dve.wait_ge(par_loaded, 80)
                dve.wait_ge(bn_rsqrt_ready, 3)
                for g_, b_, m_, isd, sc, sh in ((G1, B1, M1, ISD1, SC1, SH1), (G2, B2, M2, ISD2, SC2, SH2)):
                    step(TT(v(sc), v(isd), p(g_), ALU.mult))
                    step(TT(v(TMQ), v(sc), p(m_), ALU.mult))
                    step(TT(v(sh), p(b_), v(TMQ), ALU.subtract))
                step(TT(v(TMP), p(BIR), p(BHR), ALU.add))
                step(TS(v(BR), v(TMP), 0.5, None, ALU.mult))
                step(TT(v(TMP), p(BIZ), p(BHZ), ALU.add))
                step(TS(v(BZ), v(TMP), 0.5, None, ALU.mult))
                step(TS(v(BH), p(BHN), 0.5, None, ALU.mult))
                step(nc.vector.tensor_copy(v(BN), p(BIN)))
                dve.wait_ge(bse_spread, 1)
                step(nc.vector.tensor_copy(v(BSE), bank[2][:, 0:1]))
                step(STT(v(BL), v(BSE), con[:, KAL:KAL + 1], con[:, KCL:KCL + 1], ALU.mult, ALU.add))
                step(STT(v(BRR), v(BSE), con[:, KAR:KAR + 1], con[:, KCR:KCR + 1], ALU.mult, ALU.add))
                dve.wait_ge(small_loaded, 80)
                w = wraw[:, 0:NW * P].rearrange("p (a b) -> p a b", a=NW)
                step(nc.vector.tensor_copy(w_hi[:, :, :], w))
                step(TT(w_lo[:, :, :], w, f32(w_hi[:, :, :]), ALU.subtract))
                step(nc.vector.memset(f32(z_hi[:, :]), 0.0))
                step(nc.vector.memset(f32(z_lo[:, :]), 0.0))
                for q in range(4):
                    ws = wraw[:, NW * P:NW * P + 3]
                    cols = slice(96 + 5 * q, 99 + 5 * q)
                    step(nc.vector.tensor_copy(z_hi[:, cols], ws))
                    step(TT(z_lo[:, cols], ws, f32(z_hi[:, cols]), ALU.subtract))
                step(nc.vector.memset(f32(ones_r[:, :]), 1.0))
                step(nc.vector.tensor_copy(bmsg_r[:, :], bmsg[:, :]))
                step(STT(bmsg_r[:, :], f32(bmsg_r[:, :]), con[0:2, KNM:KNM + 1], bmsg[:, :], ALU.mult, ALU.add))
                nc.vector.memset(stats[:, :, :], 0.0).then_inc(small_ready, 1)
                nc.vector.memset(mv[:, :, :], 0.0).then_inc(vec_ready, 1)
                step(TT(bn2row[:, 3, :], bn2row[:, 2, :], bn2row[:, 0, :], ALU.mult))
                dve.wait_ge(cw_loaded, 16)
                step(TT(cwraw, cwraw, bn2row[:, 3:4, :].broadcast_to([P, TAPS, P]), ALU.mult))
                taps = cwraw[:, 0:4 * TG, :].rearrange("p (g k) o -> p g k o", k=4)
                for s, a, b in ((S01, 0, 1), (S02, 0, 2), (S13, 1, 3), (S23, 2, 3)):
                    step(TT(cwsum[:, :, s - 4, :], taps[:, :, a, :], taps[:, :, b, :], ALU.add))
                step(TT(cwsum[:, :, S0123 - 4, :], cwsum[:, :, S01 - 4, :], cwsum[:, :, S23 - 4, :], ALU.add))
                flat = EF[:, :, :].rearrange("p a b -> p (a b)")[:, 0:5 * TG * P].rearrange("p (f o) -> p f o", o=P)
                step(nc.vector.tensor_copy(cw_hi[:, 0:TAPS, :], cwraw))
                step(TT(cw_lo[:, 0:TAPS, :], cwraw, f32(cw_hi[:, 0:TAPS, :]), ALU.subtract))
                step(nc.vector.tensor_copy(cw_hi[:, TAPS:, :], flat))
                step(TT(cw_lo[:, TAPS:, :], flat, f32(cw_hi[:, TAPS:, :]), ALU.subtract))
                rows = H[:, :, :].rearrange("p c (b j) -> p c b j", b=GB)
                for c in range(PH):
                    step(nc.vector.memset(rows[:, c, :, 0:JP], 0.0))
                    step(nc.vector.memset(rows[:, c, :, JP + NI:J], 0.0))
                nc.vector.memset(rstd[:, :], 0.0).then_inc(pads_zero, 1)
                nc.vector.memset(v(TMP), 0.0).then_inc(cw_ready, 1)

            def split_x(g, k):
                dve.wait_ge(xhi_ready, 4 * g + k + 1)
                TT(chunk(x_lo, k), chunk(x, k), f32(chunk(x_hi, k)), ALU.subtract).then_inc(x_ready, 1)

            def shifted(t, a, q, n=QS):
                flat = t.rearrange("p a b -> p (a b)")
                return flat[:, a * SL + q * QS + 1:a * SL + q * QS + 1 + n]

            def differences_e(g, q):
                dve.wait_ge(h_ready, 4 * g + 2 * q + 2)
                if q == 1:
                    dve.wait_ge(vhi_ready, 2 * g + 1)
                    dve.wait_ge(v_ready, 2 * g + 1)
                cols = slice(q * QS, (q + 1) * QS)
                TT(EF[:, 0:2, :], H[:, 0:2, cols], H[:, 2:4, cols], ALU.subtract)
                for c in (2, 3):
                    last = TT(EF[:, c, :], H[:, c, cols], shifted(H[:, :, :], c - 2, q), ALU.subtract)
                last.then_inc(e_ready, 1)

            def differences_f(g, q):
                dve.wait_ge(e_ready, 2 * g + q + 1)
                ef = EF[:, :, :].rearrange("p a b -> p (a b)")
                TT(EF[:, 4:7, :], EF[:, 0:3, :], EF[:, 1:4, :], ALU.subtract)
                TT(EF[:, 7, :], EF[:, 3, :], ef[:, 1:QS + 1], ALU.subtract)
                TT(EF[:, 8, :], half(H, 2, q), half(H, 3, q), ALU.subtract)
                TT(EF[:, 9, :], half(H, 3, q), shifted(H[:, :, :], 0, q), ALU.subtract).then_inc(ef_ready, 1)

            def transformed_lo(g, q):
                dve.wait_ge(vhi_ready, 2 * g + q + 1)
                cols = slice(q * QS, (q + 1) * QS)
                TT(V_lo[:, F0:D3 + 1, cols], EF[:, 4:10, :], f32(V_hi[:, F0:D3 + 1, cols]), ALU.subtract)
                TT(V_lo[:, E1:E3 + 1, cols], EF[:, 0:4, :].rearrange("p (a two) j -> p a two j", two=2)[:, :, 1, :],
                   f32(V_hi[:, E1:E3 + 1, cols]), ALU.subtract)
                TT(half(V_lo, H3, q), half(H, 3, q), f32(half(V_hi, H3, q)), ALU.subtract).then_inc(v_ready, 1)

            def operands(g, q):
                dve.wait_ge(lrhi_ready, 2 * g + q + 1)
                STT(L[:, q, :], f32(L[:, q, :]), con[:, KNL:KNL + 1], VL[:, q, 0:N], ALU.mult, ALU.add)
                STT(R[:, q, :], f32(R[:, q, :]), con[:, KNR:KNR + 1], VR[:, q, 0:N], ALU.mult,
                    ALU.add).then_inc(lr_ready, 1)

            def mask(g, b):
                dve.wait_ge(adj_loaded[b // 2 % 2], 32 * g + 16 * (b // 4) + 16)
                dve.wait_ge(exp_ready, 8 * g + b + 1)
                TT(A[:, b % 2, :], A[:, b % 2, :], adj[:, b // 2 % 2, b % 2].rearrange("p m n -> p (m n)"),
                   ALU.mult).then_inc(a_ready, 1)

            def sums_lo(g, pair):
                dve.wait_ge(mhi_ready, 4 * g + pair + 1)
                TT(chunk(m_lo, pair), nmp_bank[pair % 2][:, :], f32(chunk(m_hi, pair)),
                   ALU.subtract).then_inc(m_ready, 1)

            def product(g, j, side, dst, grid=False):
                n = 3 * j + 1 + side
                dve.wait_ge(s_ready, 3 * g + j + 1)
                dve.wait_ge(conv2_done, 9 * g + n + 1)
                m, s = conv2_bank[n % 4][:, :], S[:, j % 2, :]
                if grid:
                    m, s = (a.rearrange("p (b i) -> p b i", b=GB) for a in (m, s))
                a0, a1 = (m, s) if side == 0 else (s, m)
                return TT(dst, a0, a1, ALU.add if side == 0 else ALU.subtract)

            def conv_sums(g):
                product(g, 0, 0, P1[:, 0, :]).then_inc(prod_used, 1)
                product(g, 0, 1, P1[:, 1, :]).then_inc(prod_used, 1)
                dve.wait_ge(prod_used, 6 * g + 2)
                p1 = P1[:, :, :].rearrange("p c (b i) -> p c b i", b=GB)
                for j in (1, 2):
                    c0 = 2 * (j - 1)
                    t = inner(c0, c0 + 2)
                    product(g, j, 0, t[:, 0], True).then_inc(prod_used, 1)
                    product(g, j, 1, t[:, 1], True).then_inc(prod_used, 1)
                    dve.wait_ge(prod_used, 6 * g + 2 * j + 2)
                    TT(t, p1, t, ALU.add if j == 1 else ALU.subtract).then_inc(t_step, 1)
                    dve.wait_ge(t_step, 2 * g + j)
                    TT(t, t, phases(x)[:, c0:c0 + 2], ALU.add).then_inc(t_ready, 1)
                    dve.wait_ge(t_ready, 2 * g + j)
                    for c in (c0, c0 + 1):
                        dve.wait_ge(chi_ready, 4 * g + c + 1)
                        STT(phases(c_lo)[:, c], inner(c, c + 1)[:, 0], 0.0, f32(phases(c_hi)[:, c]), ALU.max,
                            ALU.subtract).then_inc(c_ready, 1)

            def norm_stats(g, k):
                dve.wait_ge(turn_done, 4 * g + k + 1)
                dve.wait_ge(xn_loaded[k], 16 * g + 16)
                y = xn[:, 4 * k:4 * k + 4, :]
                STT(y, y, 4.0, turn_bank[k % 2][:, :].rearrange("p (a d) -> p a d", a=4), ALU.mult,
                    ALU.add).then_inc(y_ready, 1)
                dve.wait_ge(y_ready, 4 * g + k + 1)
                for j in range(4):
                    last = nc.vector.bn_stats(stats[:, j, :], y[:, j, :])
                last.then_inc(stats_ready, 1)

            def norm_mean():
                for j in range(4):
                    last = nc.vector.bn_aggr(mv[:, j, :], stats[:, j, :])
                last.then_inc(mv_ready, 1)

            def normalise(g, k):
                y = xn[:, 4 * k:4 * k + 4, :]
                dve.wait_ge(rstd_ready, 4 * g + k + 1)
                for j in range(4):
                    last = TS(y[:, j, :], y[:, j, :], mv[:, j, 0:1], rstd[:, j:j + 1], ALU.subtract, ALU.mult)
                last.then_inc(out_ready, 1)

            def cell(g, k):
                rk, zk, hk = r[:, k % 2, :], z[:, k % 2, :], hn[:, k % 2, :]
                dve.wait_ge(r_ready, 4 * g + k + 1)
                dve.wait_ge(hn_ready, 4 * g + k + 1)
                STT(hk, rk, 1.0, hk, ALU.add, ALU.mult).then_inc(gated_ready, 1)
                dve.wait_ge(gated_ready, 4 * g + k + 1)
                dve.wait_ge(zin_done, 4 * g + k + 1)
                TT(hk, hk, in_bank[:, :], ALU.add).then_inc(narg_ready, 1)
                if k >= 1:
                    norm_stats(g, k - 1)
                    dve.wait_ge(stats_ready, 4 * g + k)
                dve.wait_ge(n_ready, 4 * g + k + 1)
                TT(rk, chunk(x, k), hk, ALU.subtract).then_inc(e_gru_ready, 1)
                if k >= 1:
                    norm_mean()
                dve.wait_ge(e_gru_ready, 4 * g + k + 1)
                dve.wait_ge(z_ready, 4 * g + k + 1)
                STT(rk, zk, -1.0, rk, ALU.add, ALU.mult).then_inc(f_ready, 1)
                if k >= 1:
                    normalise(g, k - 1)

            def body(g, last):
                operands(g, 0)
                mask(g, 0)
                mask(g, 1)
                split_x(g, 3)
                transformed_lo(g, 0)
                mask(g, 2)
                sums_lo(g, 0)
                mask(g, 3)
                operands(g, 1)
                differences_e(g, 1)
                mask(g, 4)
                differences_f(g, 1)
                sums_lo(g, 1)
                mask(g, 5)
                mask(g, 6)
                transformed_lo(g, 1)
                sums_lo(g, 2)
                mask(g, 7)
                sums_lo(g, 3)
                conv_sums(g)
                for k in range(NC):
                    cell(g, k)
                    if not last and k >= 1:
                        split_x(g + 1, k - 1)
                norm_stats(g, NC - 1)
                dve.wait_ge(stats_ready, 4 * g + NC)
                if not last:
                    differences_e(g + 1, 0)
                norm_mean()
                if not last:
                    differences_f(g + 1, 0)
                normalise(g, NC - 1)

            setup()
            for k in range(NC - 1):
                split_x(0, k)
            differences_e(0, 0)
            differences_f(0, 0)
            with dve.Fori(0, NG - 1) as g:
                body(g, False)
            body(NG - 1, True)


def constants():
    con = np.zeros((P, NCON), np.float32)
    sel = np.zeros((P, P), np.float32)
    selb = np.zeros((3, P), np.float32)
    for q in range(4):
        for pairing in range(4):
            row = 32 * q + 5 * pairing
            con[row:row + 5, KAL] = (1, 1, 1, 1, 0)
            con[row:row + 5, KCL] = (0, 0, 0, 0, 1)
            con[row:row + 5, KAR] = (2, 2, 2, 0, -1)
            con[row:row + 5, KCR] = (0, 0, 0, -1, 0)
            con[row:row + 5, KNL] = -(pairing // 2)
            con[row:row + 5, KNR] = -(pairing % 2)
            sel[32 * q:32 * q + 3, row + 3:row + 5] = 1
            for i in range(3):
                selb[i, row + i] = 1
    con[1, KNM] = -1
    return con, sel, selb, np.eye(P, dtype=np.float32)


def kernel(**inputs):
    import concourse.bacc as bacc
    from concourse.bass_utils import run_bass_kernel_spmd

    a = {k.replace("L0_gnn_", ""): np.asarray(v) for k, v in inputs.items()}
    x, adj = a["x"], a["adj"]
    xp = x.reshape(B, NI, PH, P).transpose(0, 2, 1, 3).reshape(B, N, P)
    ap = adj.reshape(B, NI, PH, NI, PH).transpose(0, 2, 1, 4, 3).reshape(B, N, N)
    w_ih, w_hh = a["w_ih"], a["w_hh"]
    blocks = ([w_hh[i * P:(i + 1) * P].T for i in range(3)] +
              [w_ih[i * P:(i + 1) * P, :P].T for i in range(3)] +
              [w_ih[i * P:(i + 1) * P, P:].T for i in range(3)] +
              [a["conv1_w"][:, :, 0].T, a["w_msg"].T])
    b_ih, b_hh = a["b_ih"].reshape(3, P), a["b_hh"].reshape(3, P)
    par = [a["bn1_g"], a["bn1_b"], a["bn1_m"], a["bn1_v"], a["bn2_g"], a["bn2_b"], a["bn2_m"], a["bn2_v"],
           b_ih[0], b_ih[1], b_ih[2], b_hh[0], b_hh[1], b_hh[2]]
    con, sel, selb, idn = constants()
    arrays = {
        "xt": xp.reshape(NG, C, P).transpose(0, 2, 1),
        "xn": xp.reshape(NG, C // P, P, P).transpose(0, 2, 1, 3),
        "adj": ap.transpose(0, 2, 1).reshape(NG, 4, 2, MB, P, N).transpose(0, 1, 4, 2, 3, 5),
        "wsm": np.concatenate(blocks, axis=1),
        "wse": a["w_se"].T,
        "wcv": a["conv2_w"].transpose(1, 2, 0),
        "bn2": np.stack([a["bn2_g"], a["bn2_v"]]),
        "par": np.stack(par, axis=1),
        "bmsg": np.stack([a["b_msg"], a["b_msg"]]),
        "bse": a["b_se"].reshape(3, 1),
        "con": con, "sel": sel, "selb": selb, "idn": idn,
    }
    arrays = {k + "_dram": np.ascontiguousarray(v) for k, v in arrays.items()}
    nc = bacc.Bacc("TRN2", target_bir_lowering=False, num_devices=1)
    drams = [nc.dram_tensor(k, v.shape, F32, kind="ExternalInput").ap() for k, v in arrays.items()]
    out = nc.dram_tensor("out_dram", (NG, P, C // P, P), F32, kind="ExternalOutput").ap()
    build(nc, *drams, out)
    res = run_bass_kernel_spmd(nc, [arrays], core_ids=[0]).results[0]["out_dram"]
    y = res.transpose(0, 2, 1, 3).reshape(B, PH, NI, P).transpose(0, 2, 1, 3).reshape(B, N, P)
    return np.ascontiguousarray(y)
```

```python
from contextlib import ExitStack

import numpy as np

import concourse.bass as bass
from concourse import mybir

ALU = mybir.AluOpType
ACT = mybir.ActivationFunctionType
F32 = mybir.dt.float32
F32R = mybir.dt.float32r

P = 128
B = 32
N = 256
TAPS = 17
PAD = 8
EPS = 1e-5
GB = 8
NG = B // GB
C = GB * N
PH = 4
NI = N // PH
J = (N + 2 * PAD) // PH
JP = PAD // PH
CH = 512
NC = C // CH
MB = N // P
NB = CH // P
TG = TAPS // 4
SL = GB * J
QS = SL // NC
STACK = 20

D2, D3, H3, F0, F1, F2, F3, E1, E3 = range(9)
NS = 9
S01, S02, S13, S23, S0123 = range(4, 9)
NSUM = 5
PRODUCTS = [
    (H3, S0123, True), (D2, S02, True), (D3, S13, False),
    (E1, S01, True), (F0, 0, True), (F1, 1, False),
    (E3, S23, False), (F2, 2, False), (F3, 3, False),
]
NP = len(PRODUCTS)
G1, G2, B1, B2, M1, M2, V1, V2, BIR, BIZ, BHR, BHZ, BHN, BIN = range(14)
KAL, KCL, KAR, KCR, KNL, KNR, KNM = range(14, 21)
SEL, IDN = 21, 21 + P
NCST = 21 + 2 * P
ISD1, ISD2, SC1, SC2, SH1, SH2, TM1, TM2, BR, BZ, BH, BSE, BL, BRR, NSC2 = range(15)
NVEC = 15
W1, WMSG, HHR, HHZ, HHN, ICR, ICZ, ICN, IMR, IMZ, IMN = range(11)
NW = 11
NF = 3
SM = 3 + NF * P
ZW = 224


def build(nc, xt_d, xn_d, adj_d, wsm_d, wcv_d, cst_d, bmsg_d, bse_d, selb_d, out_d):
    with ExitStack() as ctx:
        def sb(name, shape, dt=F32):
            return ctx.enter_context(nc.sbuf_tensor(name, shape, dt))

        def sem(name):
            return ctx.enter_context(nc.semaphore(name))

        x = sb("x", [P, C])
        xs = sb("xs", [P, 2, CH])
        x_hi, x_lo = sb("x_hi", [P, C], F32R), sb("x_lo", [P, C], F32R)
        xn = sb("xn", [P, C // P, P])
        adj = sb("adj", [P, 2, 2, MB, N])
        H = sb("H", [P, PH, SL])
        EF = sb("EF", [P, 2, 10, QS])
        V_hi, V_lo = sb("V_hi", [P, NS, SL], F32R), sb("V_lo", [P, NS, SL], F32R)
        cw_hi = sb("cw_hi", [P, TAPS + NSUM * TG, P], F32R)
        cw_lo = sb("cw_lo", [P, TAPS + NSUM * TG, P], F32R)
        w_hl = sb("w_hl", [P, 2, NW, P], F32R)
        w_hi, w_lo = w_hl[:, 0], w_hl[:, 1]
        z_hi, z_lo = sb("z_hi", [P, ZW], F32R), sb("z_lo", [P, ZW], F32R)
        last_tap = sb("last_tap", [P, 1, P])
        cst = sb("cst", [P, NCST])
        vec = sb("vec", [P, NVEC])
        selb = sb("selb", [3, P])
        bse = sb("bse", [3, 1])
        bmsg = sb("bmsg", [2, P])
        bmsg_r = sb("bmsg_r", [2, P], F32R)
        ones_r = sb("ones_r", [2, P], F32R)
        L, R = sb("L", [P, 2, N], F32R), sb("R", [P, 2, N], F32R)
        msg = sb("msg", [P, 2, MB, P])
        m_hi, m_lo = sb("m_hi", [P, C], F32R), sb("m_lo", [P, C], F32R)
        c_hi, c_lo = sb("c_hi", [P, C], F32R), sb("c_lo", [P, C], F32R)
        r, z, hn = sb("r", [P, 2, CH]), sb("z", [P, 2, CH]), sb("hn", [P, 2, CH])
        stats = sb("stats", [P, C // P, 6])
        mv = sb("mv", [P, C // P, 2])
        rstd = sb("rstd", [P, C // P])
        pconst = sb("pconst", [P, 4])

        A = r
        VL, VR = z, hn
        ef = EF[:, :, :, :].rearrange("p u a b -> p (u a b)")
        S = ef[:, 0:2 * CH].rearrange("p (c n) -> p c n", c=2)
        P1 = ef[:, 2 * CH:4 * CH].rearrange("p (c n) -> p c n", c=2)
        w_first = hn[:, 1, 0:SM]
        w_rest = adj[:, 1, :, :, :].rearrange("p b m n -> p (b m n)")[:, 0:(NW - NF) * P]
        taps = xn
        tapsum = [x[:, i * CH:(i + 1) * CH].rearrange("p (g o) -> p g o", g=TG) for i in range(4)]
        tapsum.append(r[:, 0, :].rearrange("p (g o) -> p g o", g=TG))
        x_first = r

        bank = [ctx.enter_context(nc.psum_tensor(f"bank{i}", [P, CH], F32)) for i in range(8)]
        conv1_bank = nmp_bank = [bank[0], bank[1]]
        u_bank, dist_bank, msg_bank = [bank[2], bank[4]], [bank[3], bank[4]], bank[5]
        r_bank, z_bank, in_bank, hn_bank = bank[2], bank[3], bank[4], bank[5]
        conv2_bank = turn_bank = [bank[6], bank[7]]

        x_loaded = [sem(f"x_loaded{k}") for k in range(NC)]
        x_first_loaded = [sem(f"x_first_loaded{s}") for s in range(2)]
        xs_loaded = [sem(f"xs_loaded{s}") for s in range(2)]
        xn_loaded = [sem(f"xn_loaded{k}") for k in range(NC)]
        adj_loaded = [sem(f"adj_loaded{s}") for s in range(2)]
        out_stored = [sem(f"out_stored{k}") for k in range(NC)]
        cst_loaded, bias_loaded, taps_loaded = sem("cst_loaded"), sem("bias_loaded"), sem("taps_loaded")
        small_loaded = [sem("small_loaded0"), sem("small_loaded1")]
        pconst_ready, eps_added, pool_step = sem("pconst_ready"), sem("eps_added"), sem("pool_step")
        vec_ready, bse_spread, setup_step = sem("vec_ready"), sem("bse_spread"), sem("setup_step")
        whi_ready, small_ready, gatesw_ready = sem("whi_ready"), sem("small_ready"), sem("gatesw_ready")
        tapsum_ready, cwhi_ready, cw_ready = sem("tapsum_ready"), sem("cwhi_ready"), sem("cw_ready")
        xhi_ready, x_ready = sem("xhi_ready"), sem("x_ready")
        conv1_done, h_ready = sem("conv1_done"), sem("h_ready")
        u_done, sq_ready, usum_done = sem("u_done"), sem("sq_ready"), sem("usum_done")
        lrhi_ready, lr_ready = sem("lrhi_ready"), sem("lr_ready")
        msg_done, msg_half = sem("msg_done"), sem("msg_half")
        msg_summed, msg_ready = sem("msg_summed"), sem("msg_ready")
        dist_done, exp_ready, a_ready = sem("dist_done"), sem("exp_ready"), sem("a_ready")
        nmp_done, mhi_ready, m_ready = sem("nmp_done"), sem("mhi_ready"), sem("m_ready")
        d_ready, vahi_ready, va_ready = sem("d_ready"), sem("vahi_ready"), sem("va_ready")
        e_ready, ef_ready, vbhi_ready, vb_ready = sem("e_ready"), sem("ef_ready"), sem("vbhi_ready"), sem("vb_ready")
        conv2_done, s_ready, prod_used = sem("conv2_done"), sem("s_ready"), sem("prod_used")
        t_step, t_ready, chi_ready, c_ready = sem("t_step"), sem("t_ready"), sem("chi_ready"), sem("c_ready")
        gx_done, rhn_done, in_done, z_done = sem("gx_done"), sem("rhn_done"), sem("in_done"), sem("z_done")
        r_ready, hn_ready, z_ready, n_ready = sem("r_ready"), sem("hn_ready"), sem("z_ready"), sem("n_ready")
        gated_ready, narg_ready, diff_ready, f_ready = (
            sem("gated_ready"), sem("narg_ready"), sem("diff_ready"), sem("f_ready"))
        turn_done, y_ready = sem("turn_done"), sem("y_ready")
        stats_ready, mv_ready, rstd_ready, out_ready = (
            sem("stats_ready"), sem("mv_ready"), sem("rstd_ready"), sem("out_ready"))
        block = ctx.enter_context(nc.Block())

        def chunk(t, k):
            return t[:, k * CH:(k + 1) * CH]

        def nodes(t, b, mb):
            return t[:, b * N + mb * P:b * N + (mb + 1) * P]

        def part(t, s, k):
            return t[:, s, k * QS:(k + 1) * QS]

        def phase(t, c):
            return t[:, :].rearrange("p (b c i) -> p c b i", b=GB, c=PH)[:, c]

        def inner(c):
            return H[:, c, :].rearrange("p (b j) -> p b j", b=GB)[:, :, JP:JP + NI]

        def grid(t):
            return t.rearrange("p (b i) -> p b i", b=GB)

        def odd_e(k):
            return EF[:, k % 2, 0:4, :].rearrange("p (a two) j -> p a two j", two=2)[:, :, 1, :]

        def f32(ap):
            return ap.bitcast(F32)

        @block.sync
        def _(sp):
            def load_x(g, k):
                sp.dma_start(chunk(x, k), xt_d[g, :, k * CH:(k + 1) * CH]).then_inc(x_loaded[k], 16)

            def load_xs(g, k):
                sp.dma_start(xs[:, k % 2], xt_d[g, :, k * CH:(k + 1) * CH]).then_inc(xs_loaded[k % 2], 16)

            def load_xn(g, k):
                sp.dma_start(xn[:, NB * k:NB * k + NB, :],
                             xn_d[g, :, NB * k:NB * k + NB, :]).then_inc(xn_loaded[k], 16)

            def load_adj(g, pair):
                sp.dma_start(adj[:, pair % 2], adj_d[g, pair]).then_inc(adj_loaded[pair % 2], 16)

            def store(g, k):
                sp.wait_ge(out_ready, 4 * g + k + 1)
                sp.dma_start(out_d[g, :, NB * k:NB * k + NB, :],
                             xn[:, NB * k:NB * k + NB, :]).then_inc(out_stored[k], 16)

            def adj_rest(g):
                for pair in range(2, 4):
                    sp.wait_ge(a_ready, 8 * g + 2 * pair - 2)
                    load_adj(g, pair)

            sp.dma_start(w_first, wsm_d[:, 0:SM]).then_inc(small_loaded[0], 16)
            load_xs(0, 0)
            sp.dma_start(cst[:, :], cst_d[:, :]).then_inc(cst_loaded, 16)
            load_xs(0, 1)
            sp.dma_start(bse[:, :], bse_d[:, :]).then_inc(bias_loaded, 16)
            sp.dma_start(selb[:, :], selb_d[:, :]).then_inc(bias_loaded, 16)
            sp.dma_start(bmsg[:, :], bmsg_d[:, :]).then_inc(bias_loaded, 16)
            for k in (2, 3):
                sp.dma_start(x_first[:, k - 2], xt_d[0, :, k * CH:(k + 1) * CH]).then_inc(x_first_loaded[k - 2], 16)
            sp.dma_start(taps[:, :, :], wcv_d[:, 0:TAPS - 1, :]).then_inc(taps_loaded, 16)
            sp.dma_start(last_tap[:, :, :], wcv_d[:, TAPS - 1:TAPS, :]).then_inc(taps_loaded, 16)
            load_adj(0, 0)
            sp.dma_start(w_rest, wsm_d[:, SM:]).then_inc(small_loaded[1], 16)
            sp.wait_ge(gatesw_ready, 1)
            load_adj(0, 1)
            sp.wait_ge(cw_ready, 5)
            for k in range(NC):
                load_x(0, k)
            for k in range(NC):
                load_xn(0, k)
            adj_rest(0)
            with sp.Fori(0, NG - 1) as g:
                for s in range(2):
                    sp.wait_ge(x_ready, 4 * g + s + 3)
                    load_xs(g + 1, s)
                    sp.wait_ge(a_ready, 8 * g + 2 * s + 6)
                    load_adj(g + 1, s)
                for k in range(NC):
                    if k < 2:
                        sp.wait_ge(x_ready, 4 * g + k + 5)
                        load_xs(g + 1, k + 2)
                    sp.wait_ge(diff_ready, 4 * g + k + 1)
                    load_x(g + 1, k)
                adj_rest(g + 1)
                for k in range(NC):
                    store(g, k)
                for k in range(NC):
                    sp.wait_ge(out_stored[k], 16 * g + 16)
                    load_xn(g + 1, k)
            for k in range(NC):
                store(NG - 1, k)
            for k in range(NC):
                sp.wait_ge(out_stored[k], 16 * NG)

        @block.tensor
        def _(pe):
            def mm(out, lhs, rhs, start=False, stop=False):
                return nc.tensor.matmul(out, lhs, rhs, start=start, stop=stop, skip_group_check=True)

            def three(out, w_h, w_l, v_h, v_l, start, stop):
                mm(out, w_h, v_h, start=start)
                mm(out, w_h, v_l)
                return mm(out, w_l, v_h, stop=stop)

            def conv1(g, k):
                pe.wait_ge(x_ready, 4 * g + k + 1)
                if k >= 2:
                    pe.wait_ge(h_ready, 4 * g + k - 1)
                three(conv1_bank[k % 2][:, :], w_hi[:, W1, :], w_lo[:, W1, :], chunk(x_hi, k), chunk(x_lo, k),
                      True, True).then_inc(conv1_done, 1)

            def u_rows(g, q):
                pe.wait_ge(x_ready, 4 * g + 2 * q + 2)
                for i in range(4):
                    b = 4 * q + i
                    s = slice(96 - 32 * i, ZW - 32 * i)
                    last = three(u_bank[q][:, 0:N], z_hi[:, s], z_lo[:, s], x_hi[:, b * N:(b + 1) * N],
                                 x_lo[:, b * N:(b + 1) * N], i == 0, False)
                last.then_inc(u_done, 1)

            def u_squares(g, q):
                pe.wait_ge(sq_ready, 2 * g + q + 1)
                mm(u_bank[q][:, 0:N], cst[:, SEL:SEL + P], VL[:, q, 0:N], stop=True).then_inc(usum_done, 1)

            def messages(g, b):
                if b >= 1:
                    pe.wait_ge(msg_summed, 8 * g + b)
                pe.wait_ge(x_ready, 4 * g + b // 2 + 1)
                rows = bmsg_r[:, :].rearrange("p (o d) -> p o d", o=1).broadcast_to([2, MB, P])
                halves = msg_bank[:, :].rearrange("p (m h d) -> p m h d", m=MB, h=2)
                for mb in range(MB):
                    mm(halves[:, mb], nodes(x_hi, b, mb), w_hl[:, :, WMSG, :], start=(mb == 0))
                    mm(halves[:, mb, 0], nodes(x_lo, b, mb), w_hi[:, WMSG, :])
                mm(halves[:, :, 0], ones_r[:, :], rows, stop=True).then_inc(msg_done, 1)

            def distances(g, b):
                q, i = b // 4, b % 4
                pe.wait_ge(lr_ready, 2 * g + q + 1)
                if b >= 2:
                    pe.wait_ge(exp_ready, 8 * g + b - 1)
                elif b == 1:
                    pe.wait_ge(lrhi_ready, 2 * g + 2)
                rows = slice(32 * i, 32 * i + STACK)
                for mb in range(MB):
                    last = mm(dist_bank[b % 2][:, mb * N:(mb + 1) * N], L[rows, q, mb * P:(mb + 1) * P],
                              R[rows, q, :], start=True, stop=True)
                last.then_inc(dist_done, 1)

            def gather(g, b):
                pair = b // 2
                pe.wait_ge(msg_ready, 8 * g + b + 1)
                pe.wait_ge(a_ready, 8 * g + b + 1)
                if b % 2 == 0:
                    if pair < 2:
                        pe.wait_ge(h_ready, 4 * g + pair + 3)
                    else:
                        pe.wait_ge(m_ready, 4 * g + pair - 1)
                for mb in range(MB):
                    last = mm(nmp_bank[pair % 2][:, (b % 2) * N:(b % 2 + 1) * N], msg[:, b % 2, mb, :],
                              A[:, b % 2, mb * N:(mb + 1) * N], start=(mb == 0), stop=(mb == MB - 1))
                last.then_inc(nmp_done, 1)

            def conv2(g, n, first):
                slot, f, extra = PRODUCTS[n]
                if n == 0:
                    pe.wait_ge(va_ready, 4 * g + 4)
                if n == 3:
                    pe.wait_ge(vb_ready, 4 * g + 4)
                if first and n < 5:
                    pe.wait_ge(cw_ready, n + 1)
                if not first and n < 2:
                    pe.wait_ge(y_ready, 4 * g + n - 1)
                if n >= 2:
                    if (n - 2) % 3 == 0:
                        pe.wait_ge(s_ready, 3 * g + (n - 2) // 3 + 1)
                    else:
                        pe.wait_ge(prod_used, 6 * g + (n - 2) - (n - 2) // 3)
                for t in range(TG + extra):
                    w = 4 * t if t == TG else (4 * t + f if f < 4 else TAPS + TG * (f - 4) + t)
                    vh, vl = (V[:, slot, :].rearrange("p (b j) -> p b j", b=GB)[:, :, t:t + NI]
                              for V in (V_hi, V_lo))
                    last = three(conv2_bank[n % 2][:, :], cw_hi[:, w, :], cw_lo[:, w, :], vh, vl, t == 0,
                                 t == TG + extra - 1)
                last.then_inc(conv2_done, 1)

            def mix_stage(g, first):
                if not first:
                    pe.wait_ge(r_ready, 4 * g)
                    pe.wait_ge(hn_ready, 4 * g)
                u_rows(g, 0)
                messages(g, 0)
                if not first:
                    pe.wait_ge(narg_ready, 4 * g)
                u_rows(g, 1)
                u_squares(g, 0)
                if not first:
                    turn(g - 1, NC - 1)
                u_squares(g, 1)
                for n in range(NP):
                    conv2(g, n, first)
                    if 1 <= n < GB:
                        messages(g, n)
                    if n < GB:
                        distances(g, n)
                    if n >= 1:
                        gather(g, n - 1)

            def gates(g, k):
                xk, mk, ck = ((chunk(a, k), chunk(b, k)) for a, b in ((x_hi, x_lo), (m_hi, m_lo), (c_hi, c_lo)))

                def part(out, w, v, start=False, stop=False):
                    return three(out[:, :], w_hi[:, w, :], w_lo[:, w, :], v[0], v[1], start, stop)
                if k >= 1:
                    pe.wait_ge(r_ready, 4 * g + k)
                part(r_bank, HHR, xk, start=True)
                if k >= 1:
                    pe.wait_ge(hn_ready, 4 * g + k)
                part(hn_bank, HHN, xk, start=True, stop=True)
                if k >= 1:
                    pe.wait_ge(z_ready, 4 * g + k)
                part(z_bank, HHZ, xk, start=True).then_inc(gx_done, 1)
                if k == 0:
                    pe.wait_ge(m_ready, 4 * g + 4)
                part(r_bank, IMR, mk)
                if k >= 1:
                    part(r_bank, ICR, ck, stop=True).then_inc(rhn_done, 1)
                part(z_bank, IMZ, mk)
                if k >= 1:
                    pe.wait_ge(narg_ready, 4 * g + k)
                part(in_bank, IMN, mk, start=True)
                if k == 0:
                    pe.wait_ge(c_ready, 4 * g + 4)
                    part(r_bank, ICR, ck, stop=True).then_inc(rhn_done, 1)
                part(in_bank, ICN, ck, stop=True).then_inc(in_done, 1)
                part(z_bank, ICZ, ck, stop=True).then_inc(z_done, 1)

            def turn(g, k):
                pe.wait_ge(f_ready, 4 * g + k + 1)
                if k >= 2:
                    pe.wait_ge(y_ready, 4 * g + k - 1)
                for j in range(NB):
                    last = nc.tensor.transpose(turn_bank[k % 2][:, j * P:(j + 1) * P],
                                               r[:, k % 2, j * P:(j + 1) * P], cst[:, IDN:IDN + P])
                last.then_inc(turn_done, 1)

            def gru_stage(g, last):
                for k in range(NC):
                    gates(g, k)
                    if k >= 1:
                        turn(g, k - 1)
                    if not last:
                        conv1(g + 1, k)
                if last:
                    turn(g, NC - 1)

            pe.wait_ge(bias_loaded, 48)
            mm(bank[7][:, 0:1], selb[:, :], bse[:, :], start=True, stop=True).then_inc(bse_spread, 1)
            pe.wait_ge(small_ready, 1)
            for k in range(NC):
                conv1(0, k)
            pe.wait_ge(small_ready, 2)
            mix_stage(0, True)
            pe.wait_ge(gatesw_ready, 1)
            with pe.Fori(0, NG - 1) as g:
                gru_stage(g, False)
                mix_stage(g + 1, False)
            gru_stage(NG - 1, True)

        @block.scalar
        def _(act):
            def v(c):
                return vec[:, c:c + 1]

            def split_x(g, k, first):
                if first and k >= 2:
                    act.wait_ge(x_first_loaded[k - 2], 16)
                    src = x_first[:, k - 2]
                else:
                    act.wait_ge(xs_loaded[k % 2], 32 * g + 16 * (k // 2) + (16 if first else 0))
                    src = xs[:, k % 2]
                if not first:
                    act.wait_ge(gx_done, 4 * g + k - 3)
                nc.scalar.activation(chunk(x_hi, k), src, ACT.Copy).then_inc(xhi_ready, 1)

            def relu1(g, k):
                act.wait_ge(conv1_done, 4 * g + k + 1)
                src = conv1_bank[k % 2][:, :].rearrange("p (b c i) -> p b c i", b=2, c=PH)
                dst = H[:, :, :].rearrange("p c (b j) -> p b c j", b=GB)[:, 2 * k:2 * k + 2, :, JP:JP + NI]
                nc.scalar.activation(dst, src, ACT.Relu, bias=v(SH1), scale=v(SC1)).then_inc(h_ready, 1)

            def squares(g, q, first):
                act.wait_ge(u_done, 2 * g + q + 1)
                if first:
                    act.wait_ge(small_ready, 3)
                nc.scalar.activation(VL[:, q, 0:N], u_bank[q][:, 0:N], ACT.Square, bias=v(BSE)).then_inc(sq_ready, 1)

            def operands(g, q):
                act.wait_ge(usum_done, 2 * g + q + 1)
                u = u_bank[q][:, 0:N]
                for dst in (VL[:, q, 0:N], L[:, q, :]):
                    nc.scalar.activation(dst, u, ACT.Identity, bias=v(BL), scale=cst[:, KAL:KAL + 1])
                for dst in (VR[:, q, 0:N], R[:, q, :]):
                    last = nc.scalar.activation(dst, u, ACT.Identity, bias=v(BRR), scale=cst[:, KAR:KAR + 1])
                last.then_inc(lrhi_ready, 1)

            def message_half(g, b):
                act.wait_ge(msg_done, 8 * g + b + 1)
                if b >= 2:
                    act.wait_ge(nmp_done, 8 * g + b - 1)
                t = msg_bank[:, :].rearrange("p (m h d) -> p m h d", m=MB, h=2)
                nc.scalar.activation(msg[:, b % 2], t[:, :, 1], ACT.Copy).then_inc(msg_half, 1)

            def message(g, b):
                act.wait_ge(msg_summed, 8 * g + b + 1)
                nc.scalar.activation(msg[:, b % 2], msg[:, b % 2], ACT.Relu).then_inc(msg_ready, 1)

            def weights(g, b):
                act.wait_ge(dist_done, 8 * g + b + 1)
                nc.scalar.activation(A[:, b % 2, :], dist_bank[b % 2][:, :], ACT.Exp).then_inc(exp_ready, 1)

            def sums_hi(g, pair):
                act.wait_ge(nmp_done, 8 * g + 2 * pair + 2)
                nc.scalar.activation(chunk(m_hi, pair), nmp_bank[pair % 2][:, :], ACT.Copy).then_inc(mhi_ready, 1)

            def early_hi(g, k):
                act.wait_ge(h_ready, 4 * g + k + 1)
                nc.scalar.activation(part(V_hi, H3, k), part(H, 3, k), ACT.Copy)
                act.wait_ge(d_ready, 4 * g + k + 1)
                nc.scalar.activation(V_hi[:, D2:D3 + 1, k * QS:(k + 1) * QS], EF[:, k % 2, 8:10, :],
                                     ACT.Copy).then_inc(vahi_ready, 1)

            def late_hi(g, k):
                act.wait_ge(ef_ready, 4 * g + k + 1)
                nc.scalar.activation(V_hi[:, F0:F3 + 1, k * QS:(k + 1) * QS], EF[:, k % 2, 4:8, :], ACT.Copy)
                nc.scalar.activation(V_hi[:, E1:E3 + 1, k * QS:(k + 1) * QS], odd_e(k), ACT.Copy).then_inc(vbhi_ready, 1)

            def shared(g, j):
                act.wait_ge(conv2_done, NP * g + 3 * j + 1)
                if j == 0:
                    act.wait_ge(vb_ready, 4 * g + 3)
                if j == 2:
                    act.wait_ge(prod_used, 6 * g + 2)
                nc.scalar.activation(S[:, j % 2, :], conv2_bank[(3 * j) % 2][:, :], ACT.Identity,
                                     bias=(v(SH2) if j == 0 else 0.0), scale=v(SC2)).then_inc(s_ready, 1)

            def relu2(g, c):
                act.wait_ge(t_ready, 4 * g + c + 1)
                nc.scalar.activation(phase(c_hi, c), inner(c), ACT.Relu).then_inc(chi_ready, 1)

            def mix_head(g):
                squares(g, 0, False)
                message_half(g, 0)
                act.wait_ge(f_ready, 4 * g)
                squares(g, 1, False)
                operands(g, 0)
                message(g, 0)
                operands(g, 1)

            def mix_stage(g, first):
                for n in range(NP):
                    if n == 0 and first:
                        weights(g, 0)
                        taps_hi()
                        late_hi(g, 2)
                        late_hi(g, 3)
                        shared(g, 0)
                    elif n == 0:
                        late_hi(g, 2)
                        late_hi(g, 3)
                        weights(g, 0)
                        shared(g, 0)
                    elif n % 3 == 0 and n < NP:
                        shared(g, n // 3)
                    if n in (5, 6, 8):
                        relu2(g, {5: 0, 6: 1, 8: 2}[n])
                    if 1 <= n < GB:
                        message_half(g, n)
                        weights(g, n)
                        message(g, n)
                    if n in (2, 4, 6, 8):
                        sums_hi(g, n // 2 - 1)
                relu2(g, 3)

            def gru_stage(g, last):
                for k in range(NC):
                    if not last:
                        split_x(g + 1, k, False)
                    act.wait_ge(rhn_done, 4 * g + k + 1)
                    nc.scalar.activation(r[:, k % 2, :], r_bank[:, :], ACT.Tanh, bias=v(BR), scale=0.5).then_inc(r_ready, 1)
                    nc.scalar.activation(hn[:, k % 2, :], hn_bank[:, :], ACT.Identity, bias=v(BH),
                                         scale=0.5).then_inc(hn_ready, 1)
                    if not last and k in (1, 2):
                        late_hi(g + 1, k - 1)
                    act.wait_ge(z_done, 4 * g + k + 1)
                    nc.scalar.activation(z[:, k % 2, :], z_bank[:, :], ACT.Tanh, bias=v(BZ), scale=0.5).then_inc(z_ready, 1)
                    if not last:
                        relu1(g + 1, k)
                    act.wait_ge(narg_ready, 4 * g + k + 1)
                    nc.scalar.activation(hn[:, k % 2, :], hn[:, k % 2, :], ACT.Tanh,
                                         bias=cst[:, BIN:BIN + 1]).then_inc(n_ready, 1)
                    if not last:
                        early_hi(g + 1, k)

            act.wait_ge(small_loaded[0], 16)
            nc.scalar.activation(w_hi[:, 0:NF, :], w_first[:, 3:SM].rearrange("p (a b) -> p a b", b=P),
                                 ACT.Copy).then_inc(whi_ready, 1)
            for k in range(NC):
                split_x(0, k, True)
            act.wait_ge(vec_ready, 1)
            sums = cw_hi[:, TAPS:, :].rearrange("p (s g) o -> p s g o", g=TG)

            def sum_hi(s):
                nc.scalar.activation(sums[:, s], tapsum[s], ACT.Copy).then_inc(cwhi_ready, 1)

            def taps_hi():
                nc.scalar.activation(cw_hi[:, 0:TAPS - 1, :], taps[:, :, :], ACT.Copy).then_inc(cwhi_ready, 1)

            def gates_hi():
                act.wait_ge(small_loaded[1], 16)
                nc.scalar.activation(w_hi[:, NF:, :], w_rest.rearrange("p (a b) -> p a b", b=P),
                                     ACT.Copy).then_inc(whi_ready, 1)

            relu1(0, 0)
            for k in range(1, NC):
                relu1(0, k)
                early_hi(0, k - 1)
            early_hi(0, NC - 1)
            act.wait_ge(taps_loaded, 32)
            nc.scalar.activation(cw_hi[:, TAPS - 1:TAPS, :], last_tap[:, :, :], ACT.Copy).then_inc(cwhi_ready, 1)
            squares(0, 0, True)
            message_half(0, 0)
            squares(0, 1, True)
            act.wait_ge(tapsum_ready, 1)
            sum_hi(4)
            message(0, 0)
            operands(0, 0)
            act.wait_ge(tapsum_ready, 3)
            sum_hi(1)
            operands(0, 1)
            sum_hi(2)
            late_hi(0, 0)
            sum_hi(0)
            late_hi(0, 1)
            gates_hi()
            sum_hi(3)
            mix_stage(0, True)
            with act.Fori(0, NG - 1) as g:
                gru_stage(g, False)
                mix_head(g + 1)
                mix_stage(g + 1, False)
            gru_stage(NG - 1, True)

        @block.gpsimd
        def _(pool):
            def rsqrt(dst, src, eps, n):
                shape = [P, dst.shape[1]]
                nc.gpsimd.tensor_tensor(dst, src, eps.broadcast_to(shape), ALU.add).then_inc(eps_added, 1)
                pool.wait_ge(eps_added, n)
                return nc.gpsimd.tensor_tensor(dst, dst, pconst[:, 2:3].broadcast_to(shape), ALU.pow)

            def pair(t, c):
                return t[:, c:c + 2]

            steps = [0]

            def step(dst, a, b, op):
                nc.gpsimd.tensor_tensor(dst, a, b, op).then_inc(pool_step, 1)
                steps[0] += 1
                pool.wait_ge(pool_step, steps[0])

            for c, value in enumerate((EPS, 4.0 * EPS, -0.5, 0.5)):
                nc.gpsimd.memset(pconst[:, c:c + 1], value).then_inc(pconst_ready, 1)
            pool.wait_ge(pconst_ready, 4)
            pool.wait_ge(cst_loaded, 16)
            rsqrt(pair(vec, ISD1), pair(cst, V1), pconst[:, 0:1], 1).then_inc(eps_added, 1)
            pool.wait_ge(eps_added, 2)
            step(pair(vec, SC1), pair(vec, ISD1), pair(cst, G1), ALU.mult)
            step(pair(vec, TM1), pair(vec, SC1), pair(cst, M1), ALU.mult)
            step(pair(vec, SH1), pair(cst, B1), pair(vec, TM1), ALU.subtract)
            half_c = pconst[:, 3:4]
            step(pair(vec, TM1), pair(cst, BIR), pair(cst, BHR), ALU.add)
            step(pair(vec, BR), pair(vec, TM1), half_c.broadcast_to([P, 2]), ALU.mult)
            nc.gpsimd.tensor_tensor(vec[:, BH:BH + 1], cst[:, BHN:BHN + 1], half_c, ALU.mult).then_inc(vec_ready, 1)
            with pool.Fori(0, NG) as g:
                for k in range(NC):
                    pool.wait_ge(mv_ready, 4 * g + k + 1)
                    rsqrt(rstd[:, NB * k:NB * k + NB], mv[:, NB * k:NB * k + NB, 1], pconst[:, 1:2],
                          4 * g + k + 3).then_inc(rstd_ready, 1)

        @block.vector
        def _(dve):
            steps = [0]

            def step(ins):
                steps[0] += 1
                ins.then_inc(setup_step, 1)
                dve.wait_ge(setup_step, steps[0])

            def v(c):
                return vec[:, c:c + 1]

            def con(c, n=P):
                return cst[0:n, c:c + 1]

            TT, TS, STT = nc.vector.tensor_tensor, nc.vector.tensor_scalar, nc.vector.scalar_tensor_tensor

            def setup_small():
                rows = H[:, :, :].rearrange("p c (b j) -> p (c b) j", b=GB)
                nc.vector.memset(rows[:, :, 0:JP], 0.0)
                nc.vector.memset(rows[:, :, JP + NI:J], 0.0)
                nc.vector.memset(f32(z_hi[:, :]), 0.0)
                nc.vector.memset(f32(ones_r[:, :]), 1.0)
                step(nc.vector.memset(f32(z_lo[:, :]), 0.0))
                dve.wait_ge(whi_ready, 1)
                TT(w_lo[:, 0:NF, :], w_first[:, 3:SM].rearrange("p (a b) -> p a b", b=P), f32(w_hi[:, 0:NF, :]),
                   ALU.subtract).then_inc(small_ready, 1)

            def setup_distance():
                ws = w_first[:, 0:3].rearrange("p (o s) -> p o s", o=1).broadcast_to([P, 4, 3])
                zh, zl = (t[:, 96:116].rearrange("p (q s) -> p q s", q=4)[:, :, 0:3] for t in (z_hi, z_lo))
                nc.vector.tensor_copy(zh, ws)
                dve.wait_ge(bias_loaded, 48)
                step(nc.vector.tensor_copy(bmsg_r[:, :], bmsg[:, :]))
                TT(zl, ws, f32(zh), ALU.subtract)
                dve.wait_ge(cst_loaded, 16)
                STT(bmsg_r[:, :], f32(bmsg_r[:, :]), con(KNM, 2), bmsg[:, :], ALU.mult,
                    ALU.add).then_inc(small_ready, 1)

            def setup_bias():
                dve.wait_ge(bse_spread, 1)
                step(nc.vector.tensor_copy(v(BSE), bank[7][:, 0:1]))
                dve.wait_ge(vec_ready, 1)
                STT(v(BL), v(BSE), con(KAL), con(KCL), ALU.mult, ALU.add)
                STT(v(BRR), v(BSE), con(KAR), con(KCR), ALU.mult, ALU.add)
                TS(v(NSC2), v(SC2), -1.0, None, ALU.mult).then_inc(small_ready, 1)

            def setup_sum(i, a, b):
                t = taps[:, :, :].rearrange("p (g k) o -> p g k o", k=4)
                return TT(tapsum[i], t[:, :, a, :], t[:, :, b, :], ALU.add)

            def setup_gates_lo():
                dve.wait_ge(whi_ready, 2)
                TT(w_lo[:, NF:, :], w_rest.rearrange("p (a b) -> p a b", b=P), f32(w_hi[:, NF:, :]),
                   ALU.subtract).then_inc(gatesw_ready, 1)

            lo_sums, hi_sums = (c[:, TAPS:, :].rearrange("p (s g) o -> p s g o", g=TG) for c in (cw_lo, cw_hi))

            def setup_sum_lo(s, n):
                dve.wait_ge(cwhi_ready, n)
                return TT(lo_sums[:, s], tapsum[s], f32(hi_sums[:, s]), ALU.subtract)

            def setup_taps_lo(a, b, n):
                dve.wait_ge(cwhi_ready, n)
                src = taps[:, a:b, :] if b < TAPS else last_tap[:, :, :]
                return TT(cw_lo[:, a:b, :], src, f32(cw_hi[:, a:b, :]), ALU.subtract)

            def split_x(g, k, first):
                dve.wait_ge(xhi_ready, 4 * g + k + 1)
                src = x_first[:, k - 2] if first and k >= 2 else xs[:, k % 2]
                TT(chunk(x_lo, k), src, f32(chunk(x_hi, k)), ALU.subtract).then_inc(x_ready, 1)

            def shifted(a, n, q):
                flat = H[:, :, :].rearrange("p a b -> p (a b)")
                at = a * SL + q * QS + 1
                return flat[:, at:at + n * SL].rearrange("p (a b) -> p a b", a=n)[:, :, 0:QS]

            def early_differences(g, k):
                dve.wait_ge(h_ready, 4 * g + k + 1)
                TT(EF[:, k % 2, 8, :], part(H, 2, k), part(H, 3, k), ALU.subtract)
                TT(EF[:, k % 2, 9, :], part(H, 3, k), shifted(0, 1, k)[:, 0], ALU.subtract).then_inc(d_ready, 1)

            def early_lo(g, k):
                cols = slice(k * QS, (k + 1) * QS)
                dve.wait_ge(vahi_ready, 4 * g + k + 1)
                TT(part(V_lo, H3, k), part(H, 3, k), f32(part(V_hi, H3, k)), ALU.subtract)
                TT(V_lo[:, D2:D3 + 1, cols], EF[:, k % 2, 8:10, :], f32(V_hi[:, D2:D3 + 1, cols]),
                   ALU.subtract).then_inc(va_ready, 1)

            def late_differences_e(g, k):
                cols = slice(k * QS, (k + 1) * QS)
                TT(EF[:, k % 2, 0:2, :], H[:, 0:2, cols], H[:, 2:4, cols], ALU.subtract)
                TT(EF[:, k % 2, 2:4, :], H[:, 2:4, cols], shifted(0, 2, k), ALU.subtract).then_inc(e_ready, 1)

            def late_differences_f(g, k):
                dve.wait_ge(e_ready, 4 * g + k + 1)
                first_e = EF[:, k % 2, :, :].rearrange("p a b -> p (a b)")[:, 1:QS + 1]
                TT(EF[:, k % 2, 7, :], EF[:, k % 2, 3, :], first_e, ALU.subtract)
                TT(EF[:, k % 2, 4:7, :], EF[:, k % 2, 0:3, :], EF[:, k % 2, 1:4, :], ALU.subtract).then_inc(ef_ready, 1)

            def late_lo(g, k):
                cols = slice(k * QS, (k + 1) * QS)
                dve.wait_ge(vbhi_ready, 4 * g + k + 1)
                TT(V_lo[:, F0:F3 + 1, cols], EF[:, k % 2, 4:8, :], f32(V_hi[:, F0:F3 + 1, cols]), ALU.subtract)
                TT(V_lo[:, E1:E3 + 1, cols], odd_e(k), f32(V_hi[:, E1:E3 + 1, cols]),
                   ALU.subtract).then_inc(vb_ready, 1)

            def operands(g, q):
                dve.wait_ge(lrhi_ready, 2 * g + q + 1)
                STT(L[:, q, :], f32(L[:, q, :]), con(KNL), VL[:, q, 0:N], ALU.mult, ALU.add)
                STT(R[:, q, :], f32(R[:, q, :]), con(KNR), VR[:, q, 0:N], ALU.mult, ALU.add).then_inc(lr_ready, 1)

            def mask(g, b):
                if b % 2 == 0:
                    dve.wait_ge(adj_loaded[b // 2 % 2], 32 * g + 16 * (b // 4) + 16)
                dve.wait_ge(exp_ready, 8 * g + b + 1)
                TT(A[:, b % 2, :], A[:, b % 2, :], adj[:, b // 2 % 2, b % 2].rearrange("p m n -> p (m n)"),
                   ALU.mult).then_inc(a_ready, 1)

            def message_sum(g, b):
                dve.wait_ge(msg_half, 8 * g + b + 1)
                t = msg_bank[:, :].rearrange("p (m h d) -> p m h d", m=MB, h=2)
                TT(msg[:, b % 2], t[:, :, 0], msg[:, b % 2], ALU.add).then_inc(msg_summed, 1)

            def sums_lo(g, pair):
                dve.wait_ge(mhi_ready, 4 * g + pair + 1)
                TT(chunk(m_lo, pair), nmp_bank[pair % 2][:, :], f32(chunk(m_hi, pair)),
                   ALU.subtract).then_inc(m_ready, 1)

            def product(g, j, side):
                n = 3 * j + 1 + side
                dve.wait_ge(s_ready, 3 * g + j + 1)
                dve.wait_ge(conv2_done, NP * g + n + 1)
                if j == 0 and side == 0:
                    dve.wait_ge(vb_ready, 4 * g + 4)
                dst = grid(P1[:, side, :]) if j == 0 else inner(2 * (j - 1) + side)
                STT(dst, grid(conv2_bank[n % 2][:, :]), v(NSC2 if side else SC2), grid(S[:, j % 2, :]), ALU.mult,
                    ALU.add).then_inc(prod_used, 1)

            def conv_sum(g, c):
                j, side = 1 + c // 2, c % 2
                t, p1 = inner(c), grid(P1[:, side, :])
                dve.wait_ge(prod_used, 6 * g + 2 * j + side + 1)
                if c < 2:
                    TT(t, p1, t, ALU.add).then_inc(t_step, 1)
                    dve.wait_ge(t_step, 4 * g + 2 * c + 1)
                    TT(t, t, phase(x, c), ALU.add).then_inc(t_ready, 1)
                    TT(p1, p1, phase(x, c + 2), ALU.add).then_inc(t_step, 1)
                else:
                    dve.wait_ge(t_step, 4 * g + 2 * (c - 2) + 2)
                    TT(t, p1, t, ALU.subtract).then_inc(t_ready, 1)

            def conv_lo(g, c):
                dve.wait_ge(chi_ready, 4 * g + c + 1)
                STT(phase(c_lo, c), inner(c), 0.0, f32(phase(c_hi, c)), ALU.max, ALU.subtract).then_inc(c_ready, 1)

            def rows(k):
                return xn[:, NB * k:NB * k + NB, :]

            def residual(g, k):
                dve.wait_ge(turn_done, 4 * g + k + 1)
                dve.wait_ge(xn_loaded[k], 16 * g + 16)
                STT(rows(k), rows(k), 4.0, turn_bank[k % 2][:, :].rearrange("p (a d) -> p a d", a=NB), ALU.mult,
                    ALU.add).then_inc(y_ready, 1)

            def norm_stats(g, k):
                dve.wait_ge(y_ready, 4 * g + k + 1)
                for j in range(NB):
                    last = nc.vector.bn_stats(stats[:, NB * k + j, :], rows(k)[:, j, :])
                last.then_inc(stats_ready, 1)

            def norm_mean(k):
                for j in range(NB * k, NB * k + NB):
                    last = nc.vector.bn_aggr(mv[:, j, :], stats[:, j, :])
                last.then_inc(mv_ready, 1)

            def normalise(g, k):
                dve.wait_ge(rstd_ready, 4 * g + k + 1)
                for j in range(NB):
                    y, n = rows(k)[:, j, :], NB * k + j
                    last = TS(y, y, mv[:, n, 0:1], rstd[:, n:n + 1], ALU.subtract, ALU.mult)
                last.then_inc(out_ready, 1)

            def mix_stage(g, prev):
                def norm(what, *args):
                    if prev is not None:
                        what(*args)

                def stats_done(k):
                    norm(lambda: dve.wait_ge(stats_ready, 4 * prev + k + 1))
                first = prev is None

                def late_differences(k):
                    late_differences_e(g, k)
                    late_differences_f(g, k)
                norm(message_sum, g, 0)
                norm(residual, prev, NC - 1)
                if first:
                    late_differences(0)
                    setup_sum_lo(1, 3).then_inc(cw_ready, 1)
                    operands(g, 0)
                    late_differences(1)
                    operands(g, 1)
                    setup_sum_lo(2, 4).then_inc(cw_ready, 1)
                    late_lo(g, 0)
                    dve.wait_ge(vb_ready, 1)
                    late_differences(2)
                    late_lo(g, 1)
                else:
                    late_differences(2)
                    operands(g, 0)
                    late_differences(3)
                    late_lo(g, 2)
                mask(g, 0)
                if not first:
                    late_lo(g, 3)
                    operands(g, 1)
                if first:
                    dve.wait_ge(vb_ready, 2)
                    late_differences(3)
                    late_lo(g, 2)
                    late_lo(g, 3)
                norm(norm_stats, prev, 0)
                product(g, 0, 0)
                message_sum(g, 1)
                stats_done(0)
                mask(g, 1)
                norm(norm_mean, 0)
                if first:
                    setup_sum_lo(0, 5).then_inc(cw_ready, 1)
                    setup_gates_lo()
                norm(norm_stats, prev, 1)
                norm(norm_stats, prev, 2)
                product(g, 0, 1)
                message_sum(g, 2)
                stats_done(2)
                mask(g, 2)
                norm(norm_mean, 1)
                norm(norm_mean, 2)
                norm(normalise, prev, 0)
                if first:
                    setup_sum_lo(3, 6)
                    setup_taps_lo(0, TAPS - 1, 7).then_inc(cw_ready, 1)
                sums_lo(g, 0)
                norm(norm_stats, prev, 3)
                message_sum(g, 3)
                stats_done(3)
                mask(g, 3)
                norm(norm_mean, 3)
                norm(normalise, prev, 1)
                norm(normalise, prev, 2)
                for k in range(NC):
                    dve.wait_ge(x_loaded[k], 16 * g + 16)
                product(g, 1, 0)
                message_sum(g, 4)
                conv_sum(g, 0)
                mask(g, 4)
                norm(normalise, prev, 3)
                sums_lo(g, 1)
                product(g, 1, 1)
                message_sum(g, 5)
                mask(g, 5)
                conv_sum(g, 1)
                conv_lo(g, 0)
                message_sum(g, 6)
                mask(g, 6)
                sums_lo(g, 2)
                conv_lo(g, 1)
                product(g, 2, 0)
                message_sum(g, 7)
                conv_sum(g, 2)
                mask(g, 7)
                conv_lo(g, 2)
                product(g, 2, 1)
                conv_sum(g, 3)
                sums_lo(g, 3)
                conv_lo(g, 3)

            def gru_stage(g, last):
                for k in range(NC):
                    rk, zk, hk = r[:, k % 2, :], z[:, k % 2, :], hn[:, k % 2, :]
                    if not last and k == 0:
                        split_x(g + 1, 0, False)
                    dve.wait_ge(r_ready, 4 * g + k + 1)
                    dve.wait_ge(hn_ready, 4 * g + k + 1)
                    STT(hk, rk, 1.0, hk, ALU.add, ALU.mult).then_inc(gated_ready, 1)
                    if not last and k in (1, 2):
                        late_lo(g + 1, k - 1)
                    dve.wait_ge(gated_ready, 4 * g + k + 1)
                    dve.wait_ge(in_done, 4 * g + k + 1)
                    TT(hk, hk, in_bank[:, :], ALU.add).then_inc(narg_ready, 1)
                    if k >= 1:
                        residual(g, k - 1)
                    if not last:
                        early_differences(g + 1, k)
                    dve.wait_ge(n_ready, 4 * g + k + 1)
                    TT(rk, chunk(x, k), hk, ALU.subtract).then_inc(diff_ready, 1)
                    if not last and k < 2:
                        late_differences_e(g + 1, k)
                    dve.wait_ge(diff_ready, 4 * g + k + 1)
                    dve.wait_ge(z_ready, 4 * g + k + 1)
                    STT(rk, zk, -1.0, rk, ALU.add, ALU.mult).then_inc(f_ready, 1)
                    if last and k >= 1:
                        norm_stats(g, k - 1)
                        dve.wait_ge(stats_ready, 4 * g + k)
                        if k < NC - 1:
                            norm_mean(k - 1)
                        if k == 2:
                            normalise(g, 0)
                    if not last:
                        if k < 2:
                            late_differences_f(g + 1, k)
                        if k < NC - 1:
                            split_x(g + 1, k + 1, False)
                        early_lo(g + 1, k)
                if last:
                    residual(g, NC - 1)
                    norm_mean(NC - 2)
                    norm_stats(g, NC - 1)
                    dve.wait_ge(stats_ready, 4 * g + NC)
                    norm_mean(NC - 1)
                    for k in range(1, NC):
                        normalise(g, k)

            setup_small()
            split_x(0, 0, True)
            split_x(0, 1, True)
            setup_distance()
            split_x(0, 2, True)
            split_x(0, 3, True)
            early_differences(0, 0)
            setup_bias()
            early_differences(0, 1)
            early_lo(0, 0)
            dve.wait_ge(va_ready, 1)
            early_differences(0, 2)
            early_lo(0, 1)
            dve.wait_ge(taps_loaded, 32)
            setup_sum(0, 0, 1)
            dve.wait_ge(va_ready, 2)
            early_differences(0, 3)
            early_lo(0, 2)
            step(setup_sum(3, 2, 3))
            TT(tapsum[4], tapsum[0], tapsum[3], ALU.add).then_inc(tapsum_ready, 1)
            early_lo(0, 3)
            setup_taps_lo(TAPS - 1, TAPS, 1)
            message_sum(0, 0)
            setup_sum_lo(4, 2).then_inc(cw_ready, 1)
            setup_sum(1, 0, 2).then_inc(tapsum_ready, 1)
            setup_sum(2, 1, 3).then_inc(tapsum_ready, 1)
            mix_stage(0, None)
            with dve.Fori(0, NG - 1) as g:
                gru_stage(g, False)
                mix_stage(g + 1, g)
            gru_stage(NG - 1, True)


def constants():
    con = np.zeros((P, 7), np.float32)
    sel = np.zeros((P, P), np.float32)
    selb = np.zeros((3, P), np.float32)
    for q in range(4):
        for pairing in range(4):
            row = 32 * q + 5 * pairing
            con[row:row + 5, KAL - KAL] = (1, 1, 1, 1, 0)
            con[row:row + 5, KCL - KAL] = (0, 0, 0, 0, 1)
            con[row:row + 5, KAR - KAL] = (2, 2, 2, 0, -1)
            con[row:row + 5, KCR - KAL] = (0, 0, 0, -1, 0)
            con[row:row + 5, KNL - KAL] = -(pairing // 2)
            con[row:row + 5, KNR - KAL] = -(pairing % 2)
            sel[32 * q:32 * q + 3, row + 3:row + 5] = 1
            for i in range(3):
                selb[i, row + i] = 1
    con[1, KNM - KAL] = -1
    return con, sel, selb, np.eye(P, dtype=np.float32)


def kernel(**inputs):
    import concourse.bacc as bacc
    from concourse.bass_utils import run_bass_kernel_spmd

    a = {k.replace("L0_gnn_", ""): np.asarray(v) for k, v in inputs.items()}
    x, adj = a["x"], a["adj"]
    xp = x.reshape(B, NI, PH, P).transpose(0, 2, 1, 3).reshape(B, N, P)
    ap = adj.reshape(B, NI, PH, NI, PH).transpose(0, 2, 1, 4, 3).reshape(B, N, N)
    w_ih, w_hh = a["w_ih"], a["w_hh"]
    blocks = ([a["w_se"].T, a["conv1_w"][:, :, 0].T, a["w_msg"].T] +
              [w_hh[i * P:(i + 1) * P].T for i in range(3)] +
              [w_ih[i * P:(i + 1) * P, :P].T for i in range(3)] +
              [w_ih[i * P:(i + 1) * P, P:].T for i in range(3)])
    b_ih, b_hh = a["b_ih"].reshape(3, P), a["b_hh"].reshape(3, P)
    par = [a[f"bn{i}_{what}"] for what in "gbmv" for i in (1, 2)]
    par += [b_ih[0], b_ih[1], b_hh[0], b_hh[1], b_hh[2], b_ih[2]]
    con, sel, selb, idn = constants()
    arrays = {
        "xt": xp.reshape(NG, C, P).transpose(0, 2, 1),
        "xn": xp.reshape(NG, C // P, P, P).transpose(0, 2, 1, 3),
        "adj": ap.transpose(0, 2, 1).reshape(NG, 4, 2, MB, P, N).transpose(0, 1, 4, 2, 3, 5),
        "wsm": np.concatenate(blocks, axis=1),
        "wcv": a["conv2_w"].transpose(1, 2, 0),
        "cst": np.concatenate([np.stack(par, axis=1), con, sel, idn], axis=1),
        "bmsg": np.stack([a["b_msg"], a["b_msg"]]),
        "bse": a["b_se"].reshape(3, 1),
        "selb": selb,
    }
    arrays = {k + "_dram": np.ascontiguousarray(v) for k, v in arrays.items()}
    nc = bacc.Bacc("TRN2", target_bir_lowering=False, num_devices=1)
    drams = [nc.dram_tensor(k, v.shape, F32, kind="ExternalInput").ap() for k, v in arrays.items()]
    out = nc.dram_tensor("out_dram", (NG, P, C // P, P), F32, kind="ExternalOutput").ap()
    build(nc, *drams, out)
    res = run_bass_kernel_spmd(nc, [arrays], core_ids=[0]).results[0]["out_dram"]
    y = res.transpose(0, 2, 1, 3).reshape(B, PH, NI, P).transpose(0, 2, 1, 3).reshape(B, N, P)
    return np.ascontiguousarray(y)
```

```python
from contextlib import ExitStack

import numpy as np

import concourse.bass as bass
from concourse import mybir

ALU = mybir.AluOpType
ACT = mybir.ActivationFunctionType
F32 = mybir.dt.float32
F32R = mybir.dt.float32r

P = 128
B = 32
N = 256
TAPS = 17
PAD = 8
EPS = 1e-5
GB = 8
NG = B // GB
C = GB * N
PH = 4
NI = N // PH
J = (N + 2 * PAD) // PH
JP = PAD // PH
CH = 512
NC = C // CH
MB = N // P
NB = CH // P
TG = TAPS // 4
SL = GB * J
QS = SL // NC
STACK = 24

D2, D3, H3, F0, F1, F2, F3, E1, E3 = range(9)
NS = 9
S01, S02, S13, S23, S0123 = range(4, 9)
NSUM = 5
PRODUCTS = [
    (H3, S0123, True), (D2, S02, True), (D3, S13, False),
    (E1, S01, True), (F0, 0, True), (F1, 1, False),
    (E3, S23, False), (F2, 2, False), (F3, 3, False),
]
NP = len(PRODUCTS)
G1, G2, B1, B2, M1, M2, V1, V2, BIR, BIZ, BHR, BHZ, BHN, BIN = range(14)
KAL, KCL, KAR, KCR, KNL, KNR, KNM, KSL, KSR = range(14, 23)
IDN = 23
NCST = 23 + P
ISD1, ISD2, SC1, SC2, SH1, SH2, TM1, TM2, BR, BZ, BH, BSE, BL, BRR, NSC2 = range(15)
NVEC = 15
W1, WMSG, HHR, HHZ, HHN, ICR, ICZ, ICN, IMR, IMZ, IMN = range(11)
NW = 11
NF = 3
SM = 3 + NF * P
ZW = 224


def build(nc, xt_d, xn_d, adj_d, wsm_d, wcv_d, cst_d, bmsg_d, bse_d, selb_d, out_d):
    with ExitStack() as ctx:
        def sb(name, shape, dt=F32):
            return ctx.enter_context(nc.sbuf_tensor(name, shape, dt))

        def sem(name):
            return ctx.enter_context(nc.semaphore(name))

        x = sb("x", [P, C])
        xs = sb("xs", [P, 2, CH])
        x_hi, x_lo = sb("x_hi", [P, C], F32R), sb("x_lo", [P, C], F32R)
        xn = sb("xn", [P, C // P, P])
        adj = sb("adj", [P, 2, 2, MB, N])
        H = sb("H", [P, PH, SL])
        EF = sb("EF", [P, 2, 10, QS])
        V_hi, V_lo = sb("V_hi", [P, NS, SL], F32R), sb("V_lo", [P, NS, SL], F32R)
        cw_hi = sb("cw_hi", [P, TAPS + NSUM * TG, P], F32R)
        cw_lo = sb("cw_lo", [P, TAPS + NSUM * TG, P], F32R)
        w_hl = sb("w_hl", [P, 2, NW, P], F32R)
        w_hi, w_lo = w_hl[:, 0], w_hl[:, 1]
        z_hi, z_lo = sb("z_hi", [P, ZW], F32R), sb("z_lo", [P, ZW], F32R)
        last_tap = sb("last_tap", [P, 1, P])
        cst = sb("cst", [P, NCST])
        vec = sb("vec", [P, NVEC])
        selb = sb("selb", [3, P])
        bse = sb("bse", [3, 1])
        bmsg = sb("bmsg", [2, P])
        bmsg_r = sb("bmsg_r", [2, P], F32R)
        ones_r = sb("ones_r", [2, P], F32R)
        L, R = sb("L", [P, 2, N], F32R), sb("R", [P, 2, N], F32R)
        msg = sb("msg", [P, 2, MB, P])
        m_hi, m_lo = sb("m_hi", [P, C], F32R), sb("m_lo", [P, C], F32R)
        c_hi, c_lo = sb("c_hi", [P, C], F32R), sb("c_lo", [P, C], F32R)
        r, z, hn = sb("r", [P, 2, CH]), sb("z", [P, 2, CH]), sb("hn", [P, 2, CH])
        stats = sb("stats", [P, C // P, 6])
        mv = sb("mv", [P, C // P, 2])
        rstd = sb("rstd", [P, C // P])
        shift = sb("shift", [P, NB])
        pconst = sb("pconst", [P, 5])

        A = r
        VL, VR = z, hn
        SQ = z[:, :, N:2 * N]
        ef = EF[:, :, :, :].rearrange("p u a b -> p (u a b)")
        P1_first = xs
        P1_later = ef[:, 2 * CH:4 * CH].rearrange("p (c n) -> p c n", c=2)
        S_later = [hn[:, :, N:2 * N]] + [ef[:, (j % 2) * CH:(j % 2 + 1) * CH] for j in (1, 2)]
        S_first = [x[:, CH:2 * CH], ef[:, SL:SL + CH], ef[:, 0:CH]]
        E_all = ef[:, 0:4 * SL].rearrange("p (c j) -> p c j", c=4)
        F_one = ef[:, 4 * SL:5 * SL]
        w_first = hn[:, 1, 0:SM]
        w_rest = adj[:, 1, :, :, :].rearrange("p b m n -> p (b m n)")[:, 0:(NW - NF) * P]
        taps = xn
        tapsum = [x[:, i * CH:(i + 1) * CH].rearrange("p (g o) -> p g o", g=TG) for i in range(4)]
        tapsum.append(r[:, 0, :].rearrange("p (g o) -> p g o", g=TG))
        x_first = r

        bank = [ctx.enter_context(nc.psum_tensor(f"bank{i}", [P, CH], F32)) for i in range(8)]
        conv1_bank = nmp_bank = [bank[0], bank[1]]
        u_bank, dist_bank, msg_bank = [bank[2], bank[4]], [bank[3], bank[4]], bank[5]
        r_bank, z_bank, in_bank, hn_bank = bank[2], bank[3], bank[4], bank[5]
        conv2_bank = turn_bank = [bank[6], bank[7]]

        x_loaded = [sem(f"x_loaded{k}") for k in range(NC)]
        x_first_loaded = [sem(f"x_first_loaded{s}") for s in range(2)]
        xs_loaded = [sem(f"xs_loaded{s}") for s in range(2)]
        xn_loaded = [sem(f"xn_loaded{k}") for k in range(NC)]
        adj_loaded = [sem(f"adj_loaded{s}") for s in range(2)]
        out_stored = [sem(f"out_stored{k}") for k in range(NC)]
        cst_loaded, bias_loaded, taps_loaded = sem("cst_loaded"), sem("bias_loaded"), sem("taps_loaded")
        small_loaded = [sem("small_loaded0"), sem("small_loaded1")]
        pconst_ready, eps_added, pool_step = sem("pconst_ready"), sem("eps_added"), sem("pool_step")
        vec_ready, bse_spread, setup_step = sem("vec_ready"), sem("bse_spread"), sem("setup_step")
        whi_ready, small_ready, gatesw_ready = sem("whi_ready"), sem("small_ready"), sem("gatesw_ready")
        tapsum_ready, cwhi_ready, cw_ready = sem("tapsum_ready"), sem("cwhi_ready"), sem("cw_ready")
        xhi_ready, x_ready = sem("xhi_ready"), sem("x_ready")
        conv1_done, h_ready = sem("conv1_done"), sem("h_ready")
        u_done, affine_ready, rows_ready = sem("u_done"), sem("affine_ready"), sem("rows_ready")
        lrhi_ready, lr_ready = sem("lrhi_ready"), sem("lr_ready")
        msg_done, msg_half = sem("msg_done"), sem("msg_half")
        msg_summed, msg_ready = sem("msg_summed"), sem("msg_ready")
        dist_done, exp_ready, a_ready = sem("dist_done"), sem("exp_ready"), sem("a_ready")
        nmp_done, mhi_ready, m_ready = sem("nmp_done"), sem("mhi_ready"), sem("m_ready")
        d_ready, vahi_ready, va_ready = sem("d_ready"), sem("vahi_ready"), sem("va_ready")
        e_ready, ef_ready, vbhi_ready, vb_ready = sem("e_ready"), sem("ef_ready"), sem("vbhi_ready"), sem("vb_ready")
        sum23_ready = sem("sum23_ready")
        slot_diff, slot_hi, slot_lo = sem("slot_diff"), sem("slot_hi"), sem("slot_lo")
        conv2_done, s_ready, prod_used = sem("conv2_done"), sem("s_ready"), sem("prod_used")
        t_step, t_ready, chi_ready, c_ready = sem("t_step"), sem("t_ready"), sem("chi_ready"), sem("c_ready")
        gx_done, rhn_done, in_done, z_done = sem("gx_done"), sem("rhn_done"), sem("in_done"), sem("z_done")
        r_ready, hn_ready, z_ready, n_ready = sem("r_ready"), sem("hn_ready"), sem("z_ready"), sem("n_ready")
        gated_ready, narg_ready, diff_ready, f_ready = (
            sem("gated_ready"), sem("narg_ready"), sem("diff_ready"), sem("f_ready"))
        shift_ready, act_out_ready = sem("shift_ready"), sem("act_out_ready")
        turn_done, y_ready = sem("turn_done"), sem("y_ready")
        stats_ready, mv_ready, rstd_ready, out_ready = (
            sem("stats_ready"), sem("mv_ready"), sem("rstd_ready"), sem("out_ready"))
        block = ctx.enter_context(nc.Block())

        def chunk(t, k):
            return t[:, k * CH:(k + 1) * CH]

        def nodes(t, b, mb):
            return t[:, b * N + mb * P:b * N + (mb + 1) * P]

        def part(t, s, k):
            return t[:, s, k * QS:(k + 1) * QS]

        def phase(t, c):
            return t[:, :].rearrange("p (b c i) -> p c b i", b=GB, c=PH)[:, c]

        def inner(c):
            return H[:, c, :].rearrange("p (b j) -> p b j", b=GB)[:, :, JP:JP + NI]

        def grid(t):
            return t.rearrange("p (b i) -> p b i", b=GB)

        def odd_e(k):
            return EF[:, k % 2, 0:4, :].rearrange("p (a two) j -> p a two j", two=2)[:, :, 1, :]

        def f32(ap):
            return ap.bitcast(F32)

        @block.sync
        def _(sp):
            def load_x(g, k):
                sp.dma_start(chunk(x, k), xt_d[g, :, k * CH:(k + 1) * CH]).then_inc(x_loaded[k], 16)

            def load_xs(g, k):
                sp.dma_start(xs[:, k % 2], xt_d[g, :, k * CH:(k + 1) * CH]).then_inc(xs_loaded[k % 2], 16)

            def load_xn(g, k):
                sp.dma_start(xn[:, NB * k:NB * k + NB, :],
                             xn_d[g, :, NB * k:NB * k + NB, :]).then_inc(xn_loaded[k], 16)

            def load_adj(g, pair):
                sp.dma_start(adj[:, pair % 2], adj_d[g, pair]).then_inc(adj_loaded[pair % 2], 16)

            def store(g, k, last=False):
                if not last:
                    sp.wait_ge(out_ready, 4 * g + k + 1)
                elif k == 1:
                    sp.wait_ge(act_out_ready, 1)
                else:
                    sp.wait_ge(out_ready, 4 * g + k + (1 if k == 0 else 0))
                sp.dma_start(out_d[g, :, NB * k:NB * k + NB, :],
                             xn[:, NB * k:NB * k + NB, :]).then_inc(out_stored[k], 16)

            def load_adj_late(g, pair):
                sp.wait_ge(a_ready, 8 * g + 2 * pair - 2)
                load_adj(g, pair)

            sp.dma_start(w_first, wsm_d[:, 0:SM]).then_inc(small_loaded[0], 16)
            load_xs(0, 0)
            sp.dma_start(cst[:, :], cst_d[:, :]).then_inc(cst_loaded, 16)
            load_xs(0, 1)
            sp.dma_start(bse[:, :], bse_d[:, :]).then_inc(bias_loaded, 16)
            sp.dma_start(selb[:, :], selb_d[:, :]).then_inc(bias_loaded, 16)
            sp.dma_start(bmsg[:, :], bmsg_d[:, :]).then_inc(bias_loaded, 16)
            for k in (2, 3):
                sp.dma_start(x_first[:, k - 2], xt_d[0, :, k * CH:(k + 1) * CH]).then_inc(x_first_loaded[k - 2], 16)
            sp.dma_start(taps[:, :, :], wcv_d[:, 0:TAPS - 1, :]).then_inc(taps_loaded, 16)
            sp.dma_start(last_tap[:, :, :], wcv_d[:, TAPS - 1:TAPS, :]).then_inc(taps_loaded, 16)
            load_adj(0, 0)
            sp.dma_start(w_rest, wsm_d[:, SM:]).then_inc(small_loaded[1], 16)
            sp.wait_ge(gatesw_ready, 1)
            load_adj(0, 1)
            load_adj_late(0, 2)
            sp.wait_ge(sum23_ready, 1)
            for k in range(NC):
                load_x(0, k)
            load_adj_late(0, 3)
            sp.wait_ge(cw_ready, NP - 1)
            for k in range(NC):
                load_xn(0, k)
            with sp.Fori(0, NG - 1) as g:
                sp.wait_ge(t_ready, 4)
                for s in range(2):
                    sp.wait_ge(x_ready, 4 * g + s + 3)
                    load_xs(g + 1, s)
                    sp.wait_ge(a_ready, 8 * g + 2 * s + 6)
                    load_adj(g + 1, s)
                for k in range(NC):
                    if k < 2:
                        sp.wait_ge(x_ready, 4 * g + k + 5)
                        load_xs(g + 1, k + 2)
                    sp.wait_ge(diff_ready, 4 * g + k + 1)
                    load_x(g + 1, k)
                for pair in range(2, 4):
                    load_adj_late(g + 1, pair)
                for k in range(NC):
                    store(g, k)
                for k in range(NC):
                    sp.wait_ge(out_stored[k], 16 * g + 16)
                    load_xn(g + 1, k)
            for k in range(NC):
                store(NG - 1, k, True)
            for k in range(NC):
                sp.wait_ge(out_stored[k], 16 * NG)

        @block.tensor
        def _(pe):
            def mm(out, lhs, rhs, start=False, stop=False):
                return nc.tensor.matmul(out, lhs, rhs, start=start, stop=stop, skip_group_check=True)

            def three(out, w_h, w_l, v_h, v_l, start, stop):
                mm(out, w_h, v_h, start=start)
                mm(out, w_h, v_l)
                return mm(out, w_l, v_h, stop=stop)

            def conv1(g, k):
                pe.wait_ge(x_ready, 4 * g + k + 1)
                if k >= 2:
                    pe.wait_ge(h_ready, 4 * g + k - 1)
                three(conv1_bank[k % 2][:, :], w_hi[:, W1, :], w_lo[:, W1, :], chunk(x_hi, k), chunk(x_lo, k),
                      True, True).then_inc(conv1_done, 1)

            def u_rows(g, q):
                pe.wait_ge(x_ready, 4 * g + 2 * q + 2)
                for i in range(4):
                    b = 4 * q + i
                    s = slice(96 - 32 * i, ZW - 32 * i)
                    last = three(u_bank[q][:, 0:N], z_hi[:, s], z_lo[:, s], x_hi[:, b * N:(b + 1) * N],
                                 x_lo[:, b * N:(b + 1) * N], i == 0, i == 3)
                last.then_inc(u_done, 1)

            def messages(g, b):
                if b >= 1:
                    pe.wait_ge(msg_summed, 8 * g + b)
                pe.wait_ge(x_ready, 4 * g + b // 2 + 1)
                rows = bmsg_r[:, :].rearrange("p (o d) -> p o d", o=1).broadcast_to([2, MB, P])
                halves = msg_bank[:, :].rearrange("p (m h d) -> p m h d", m=MB, h=2)
                for mb in range(MB):
                    mm(halves[:, mb], nodes(x_hi, b, mb), w_hl[:, :, WMSG, :], start=(mb == 0))
                    mm(halves[:, mb, 0], nodes(x_lo, b, mb), w_hi[:, WMSG, :])
                mm(halves[:, :, 0], ones_r[:, :], rows, stop=True).then_inc(msg_done, 1)

            def distances(g, b):
                q, i = b // 4, b % 4
                pe.wait_ge(lr_ready, 2 * g + q + 1)
                if b >= 2:
                    pe.wait_ge(exp_ready, 8 * g + b - 1)
                elif b == 1:
                    pe.wait_ge(lrhi_ready, 2 * g + 2)
                rows = slice(32 * i, 32 * i + STACK)
                for mb in range(MB):
                    last = mm(dist_bank[b % 2][:, mb * N:(mb + 1) * N], L[rows, q, mb * P:(mb + 1) * P],
                              R[rows, q, :], start=True, stop=True)
                last.then_inc(dist_done, 1)

            def gather(g, b):
                pair = b // 2
                pe.wait_ge(msg_ready, 8 * g + b + 1)
                pe.wait_ge(a_ready, 8 * g + b + 1)
                if b % 2 == 0:
                    if pair < 2:
                        pe.wait_ge(h_ready, 4 * g + pair + 3)
                    else:
                        pe.wait_ge(m_ready, 4 * g + pair - 1)
                for mb in range(MB):
                    last = mm(nmp_bank[pair % 2][:, (b % 2) * N:(b % 2 + 1) * N], msg[:, b % 2, mb, :],
                              A[:, b % 2, mb * N:(mb + 1) * N], start=(mb == 0), stop=(mb == MB - 1))
                last.then_inc(nmp_done, 1)

            def conv2(g, n, first):
                slot, f, extra = PRODUCTS[n]
                if n == 0:
                    pe.wait_ge(va_ready, 4 * g + 4)
                if first and n >= 3:
                    pe.wait_ge(slot_lo, n - 2)
                elif n == 3:
                    pe.wait_ge(vb_ready, 4 * g)
                if first and n == 6:
                    pe.wait_ge(sum23_ready, 1)
                elif first:
                    pe.wait_ge(cw_ready, n + 1 if n < 6 else n)
                if not first and n < 2:
                    pe.wait_ge(y_ready, 4 * g + n - 1)
                if n >= 2:
                    if (n - 2) % 3 == 0:
                        pe.wait_ge(s_ready, 3 * g + (n - 2) // 3 + 1)
                    else:
                        pe.wait_ge(prod_used, 6 * g + (n - 2) - (n - 2) // 3)
                for t in range(TG + extra):
                    w = 4 * t if t == TG else (4 * t + f if f < 4 else TAPS + TG * (f - 4) + t)
                    vh, vl = (V[:, slot, :].rearrange("p (b j) -> p b j", b=GB)[:, :, t:t + NI]
                              for V in (V_hi, V_lo))
                    last = three(conv2_bank[n % 2][:, :], cw_hi[:, w, :], cw_lo[:, w, :], vh, vl, t == 0,
                                 t == TG + extra - 1)
                last.then_inc(conv2_done, 1)

            def mix_stage(g, first):
                if not first:
                    pe.wait_ge(r_ready, 4 * g)
                    pe.wait_ge(hn_ready, 4 * g)
                u_rows(g, 0)
                messages(g, 0)
                if not first:
                    pe.wait_ge(narg_ready, 4 * g)
                else:
                    pe.wait_ge(va_ready, 3)
                u_rows(g, 1)
                if not first:
                    turn(g - 1, NC - 1)
                for n in range(NP):
                    conv2(g, n, first)
                    if 1 <= n < GB:
                        messages(g, n)
                    if n < GB:
                        distances(g, n)
                    if n >= 1:
                        gather(g, n - 1)

            def gates(g, k):
                xk, mk, ck = ((chunk(a, k), chunk(b, k)) for a, b in ((x_hi, x_lo), (m_hi, m_lo), (c_hi, c_lo)))

                def part(out, w, v, start=False, stop=False):
                    return three(out[:, :], w_hi[:, w, :], w_lo[:, w, :], v[0], v[1], start, stop)
                if k >= 1:
                    pe.wait_ge(r_ready, 4 * g + k)
                part(r_bank, HHR, xk, start=True)
                if k >= 1:
                    pe.wait_ge(hn_ready, 4 * g + k)
                part(hn_bank, HHN, xk, start=True, stop=True)
                if k >= 1:
                    pe.wait_ge(z_ready, 4 * g + k)
                part(z_bank, HHZ, xk, start=True).then_inc(gx_done, 1)
                if k == 0:
                    pe.wait_ge(m_ready, 4 * g + 4)
                part(r_bank, IMR, mk)
                if k >= 1:
                    part(r_bank, ICR, ck, stop=True).then_inc(rhn_done, 1)
                part(z_bank, IMZ, mk)
                if k >= 1:
                    pe.wait_ge(narg_ready, 4 * g + k)
                part(in_bank, IMN, mk, start=True)
                if k == 0:
                    pe.wait_ge(c_ready, 4 * g + 4)
                    part(r_bank, ICR, ck, stop=True).then_inc(rhn_done, 1)
                part(in_bank, ICN, ck, stop=True).then_inc(in_done, 1)
                part(z_bank, ICZ, ck, stop=True).then_inc(z_done, 1)

            def turn(g, k):
                pe.wait_ge(f_ready, 4 * g + k + 1)
                if k >= 2:
                    pe.wait_ge(y_ready, 4 * g + k - 1)
                for j in range(NB):
                    last = nc.tensor.transpose(turn_bank[k % 2][:, j * P:(j + 1) * P],
                                               r[:, k % 2, j * P:(j + 1) * P], cst[:, IDN:IDN + P])
                last.then_inc(turn_done, 1)

            def gru_stage(g, last):
                for k in range(NC):
                    gates(g, k)
                    if k >= 1:
                        turn(g, k - 1)
                    if not last:
                        conv1(g + 1, k)
                if last:
                    turn(g, NC - 1)

            pe.wait_ge(bias_loaded, 48)
            mm(bank[7][:, 0:1], selb[:, :], bse[:, :], start=True, stop=True).then_inc(bse_spread, 1)
            pe.wait_ge(small_ready, 1)
            for k in range(NC):
                conv1(0, k)
            pe.wait_ge(small_ready, 2)
            mix_stage(0, True)
            pe.wait_ge(gatesw_ready, 1)
            with pe.Fori(0, NG - 1) as g:
                gru_stage(g, False)
                mix_stage(g + 1, False)
            gru_stage(NG - 1, True)

        @block.scalar
        def _(act):
            def v(c):
                return vec[:, c:c + 1]

            def split_x(g, k, first):
                if first and k >= 2:
                    act.wait_ge(x_first_loaded[k - 2], 16)
                    src = x_first[:, k - 2]
                else:
                    act.wait_ge(xs_loaded[k % 2], 32 * g + 16 * (k // 2) + (16 if first else 0))
                    src = xs[:, k % 2]
                if not first:
                    act.wait_ge(gx_done, 4 * g + k - 3)
                nc.scalar.activation(chunk(x_hi, k), src, ACT.Copy).then_inc(xhi_ready, 1)

            def relu1(g, k):
                act.wait_ge(conv1_done, 4 * g + k + 1)
                src = conv1_bank[k % 2][:, :].rearrange("p (b c i) -> p b c i", b=2, c=PH)
                dst = H[:, :, :].rearrange("p c (b j) -> p b c j", b=GB)[:, 2 * k:2 * k + 2, :, JP:JP + NI]
                nc.scalar.activation(dst, src, ACT.Relu, bias=v(SH1), scale=v(SC1)).then_inc(h_ready, 1)

            def affine(g, q, first):
                act.wait_ge(u_done, 2 * g + q + 1)
                if first:
                    act.wait_ge(small_ready, 3)
                u = u_bank[q][:, 0:N]
                nc.scalar.activation(SQ[:, q], u, ACT.Square, bias=v(BSE))
                nc.scalar.activation(VL[:, q, 0:N], u, ACT.Identity, bias=v(BL), scale=cst[:, KAL:KAL + 1])
                nc.scalar.activation(VR[:, q, 0:N], u, ACT.Identity, bias=v(BRR),
                                     scale=cst[:, KAR:KAR + 1]).then_inc(affine_ready, 1)

            def operands(g, q):
                act.wait_ge(rows_ready, 2 * g + q + 1)
                nc.scalar.activation(L[:, q, :], VL[:, q, 0:N], ACT.Copy)
                nc.scalar.activation(R[:, q, :], VR[:, q, 0:N], ACT.Copy).then_inc(lrhi_ready, 1)

            def message_half(g, b):
                act.wait_ge(msg_done, 8 * g + b + 1)
                if b >= 2:
                    act.wait_ge(nmp_done, 8 * g + b - 1)
                t = msg_bank[:, :].rearrange("p (m h d) -> p m h d", m=MB, h=2)
                nc.scalar.activation(msg[:, b % 2], t[:, :, 1], ACT.Copy).then_inc(msg_half, 1)

            def message(g, b):
                act.wait_ge(msg_summed, 8 * g + b + 1)
                nc.scalar.activation(msg[:, b % 2], msg[:, b % 2], ACT.Relu).then_inc(msg_ready, 1)

            def weights(g, b):
                act.wait_ge(dist_done, 8 * g + b + 1)
                nc.scalar.activation(A[:, b % 2, :], dist_bank[b % 2][:, :], ACT.Exp).then_inc(exp_ready, 1)

            def sums_hi(g, pair):
                act.wait_ge(nmp_done, 8 * g + 2 * pair + 2)
                nc.scalar.activation(chunk(m_hi, pair), nmp_bank[pair % 2][:, :], ACT.Copy).then_inc(mhi_ready, 1)

            def early_hi(g, k):
                act.wait_ge(h_ready, 4 * g + k + 1)
                nc.scalar.activation(part(V_hi, H3, k), part(H, 3, k), ACT.Copy)
                act.wait_ge(d_ready, 4 * g + k + 1)
                nc.scalar.activation(V_hi[:, D2:D3 + 1, k * QS:(k + 1) * QS], EF[:, k % 2, 8:10, :],
                                     ACT.Copy).then_inc(vahi_ready, 1)

            def slot_high(slot, src, n):
                act.wait_ge(slot_diff, n)
                nc.scalar.activation(V_hi[:, slot, :], src, ACT.Copy).then_inc(slot_hi, 1)

            def late_hi(g, k):
                act.wait_ge(ef_ready, 4 * g + k - 3)
                nc.scalar.activation(V_hi[:, F0:F3 + 1, k * QS:(k + 1) * QS], EF[:, k % 2, 4:8, :], ACT.Copy)
                nc.scalar.activation(V_hi[:, E1:E3 + 1, k * QS:(k + 1) * QS], odd_e(k), ACT.Copy).then_inc(vbhi_ready, 1)

            def shared(g, j, first):
                act.wait_ge(conv2_done, NP * g + 3 * j + 1)
                if j == 2:
                    act.wait_ge(prod_used, 6 * g + 2)
                if first:
                    act.wait_ge(*((cw_ready, 2), (slot_diff, 4), (slot_lo, 6))[j])
                src, dst = conv2_bank[(3 * j) % 2][:, :], (S_first if first else S_later)[j]
                if not first and j == 0:
                    src = src.rearrange("p (h n) -> p h n", h=2)
                nc.scalar.activation(dst, src, ACT.Identity,
                                     bias=(v(SH2) if j == 0 else 0.0), scale=v(SC2)).then_inc(s_ready, 1)

            def relu2(g, c):
                act.wait_ge(t_ready, 4 * g + c + 1)
                nc.scalar.activation(phase(c_hi, c), inner(c), ACT.Relu).then_inc(chi_ready, 1)

            def mix_head(g):
                affine(g, 0, False)
                message_half(g, 0)
                act.wait_ge(f_ready, 4 * g)
                affine(g, 1, False)
                operands(g, 0)
                message(g, 0)
                operands(g, 1)

            def mix_stage(g, first):
                for n in range(NP):
                    if n == 0 and first:
                        slot_high(E1, E_all[:, 1], 1)
                        shared(g, 0, first)
                        weights(g, 0)
                        sum_hi(0)
                        sum_hi(3)
                        gates_hi()
                        slot_high(F0, F_one, 2)
                    elif n == 0:
                        late_hi(g, 2)
                        weights(g, 0)
                        late_hi(g, 3)
                        shared(g, 0, first)
                    elif n % 3 == 0 and n < NP:
                        shared(g, n // 3, first)
                    if n in (5, 6, 8):
                        relu2(g, {5: 0, 6: 1, 8: 2}[n])
                    if 1 <= n < GB:
                        message_half(g, n)
                        weights(g, n)
                        if first and n == 3:
                            slot_high(E3, E_all[:, 3], 3)
                            slot_high(F2, F_one, 4)
                        if first and n == 4:
                            slot_high(F3, F_one, 5)
                        message(g, n)
                    if n in (2, 4, 6, 8):
                        sums_hi(g, n // 2 - 1)
                    if first and n == 1:
                        taps_hi()
                        slot_high(F1, F_one, 3)
                relu2(g, 3)

            def normalise_one(k):
                act.wait_ge(shift_ready, 1)
                for j in range(NB * k, NB * k + NB):
                    last = nc.scalar.activation(xn[:, j, :], xn[:, j, :], ACT.Identity, bias=shift[:, j - NB * k:j - NB * k + 1],
                                                scale=rstd[:, j:j + 1])
                last.then_inc(act_out_ready, 1)

            def gru_stage(g, last):
                for k in range(NC):
                    if not last:
                        split_x(g + 1, k, False)
                    act.wait_ge(rhn_done, 4 * g + k + 1)
                    nc.scalar.activation(r[:, k % 2, :], r_bank[:, :], ACT.Tanh, bias=v(BR), scale=0.5).then_inc(r_ready, 1)
                    nc.scalar.activation(hn[:, k % 2, :], hn_bank[:, :], ACT.Identity, bias=v(BH),
                                         scale=0.5).then_inc(hn_ready, 1)
                    if not last and k in (1, 2):
                        late_hi(g + 1, k - 1)
                    act.wait_ge(z_done, 4 * g + k + 1)
                    nc.scalar.activation(z[:, k % 2, :], z_bank[:, :], ACT.Tanh, bias=v(BZ), scale=0.5).then_inc(z_ready, 1)
                    if not last:
                        relu1(g + 1, k)
                    act.wait_ge(narg_ready, 4 * g + k + 1)
                    nc.scalar.activation(hn[:, k % 2, :], hn[:, k % 2, :], ACT.Tanh,
                                         bias=cst[:, BIN:BIN + 1]).then_inc(n_ready, 1)
                    if not last:
                        early_hi(g + 1, k)
                if last:
                    normalise_one(1)

            act.wait_ge(small_loaded[0], 16)
            nc.scalar.activation(w_hi[:, 0:NF, :], w_first[:, 3:SM].rearrange("p (a b) -> p a b", b=P),
                                 ACT.Copy).then_inc(whi_ready, 1)
            for k in range(NC):
                split_x(0, k, True)
            act.wait_ge(vec_ready, 1)
            sums = cw_hi[:, TAPS:, :].rearrange("p (s g) o -> p s g o", g=TG)

            def sum_hi(s):
                nc.scalar.activation(sums[:, s], tapsum[s], ACT.Copy).then_inc(cwhi_ready, 1)

            def taps_hi():
                nc.scalar.activation(cw_hi[:, 0:TAPS - 1, :], taps[:, :, :], ACT.Copy).then_inc(cwhi_ready, 1)

            def gates_hi():
                act.wait_ge(small_loaded[1], 16)
                nc.scalar.activation(w_hi[:, NF:, :], w_rest.rearrange("p (a b) -> p a b", b=P),
                                     ACT.Copy).then_inc(whi_ready, 1)

            relu1(0, 0)
            for k in range(1, NC):
                relu1(0, k)
                early_hi(0, k - 1)
            early_hi(0, NC - 1)
            act.wait_ge(taps_loaded, 32)
            nc.scalar.activation(cw_hi[:, TAPS - 1:TAPS, :], last_tap[:, :, :], ACT.Copy).then_inc(cwhi_ready, 1)
            affine(0, 0, True)
            act.wait_ge(tapsum_ready, 1)
            sum_hi(4)
            message_half(0, 0)
            affine(0, 1, True)
            operands(0, 0)
            message(0, 0)
            act.wait_ge(tapsum_ready, 3)
            sum_hi(1)
            operands(0, 1)
            sum_hi(2)
            mix_stage(0, True)
            with act.Fori(0, NG - 1) as g:
                gru_stage(g, False)
                mix_head(g + 1)
                mix_stage(g + 1, False)
            gru_stage(NG - 1, True)

        @block.gpsimd
        def _(pool):
            def rsqrt(dst, src, eps, n):
                shape = [P, dst.shape[1]]
                nc.gpsimd.tensor_tensor(dst, src, eps.broadcast_to(shape), ALU.add).then_inc(eps_added, 1)
                pool.wait_ge(eps_added, n)
                return nc.gpsimd.tensor_tensor(dst, dst, pconst[:, 2:3].broadcast_to(shape), ALU.pow)

            def pair(t, c):
                return t[:, c:c + 2]

            steps = [0]

            def step(dst, a, b, op):
                nc.gpsimd.tensor_tensor(dst, a, b, op).then_inc(pool_step, 1)
                steps[0] += 1
                pool.wait_ge(pool_step, steps[0])

            for c, value in enumerate((EPS, 4.0 * EPS, -0.5, 0.5, -1.0)):
                nc.gpsimd.memset(pconst[:, c:c + 1], value).then_inc(pconst_ready, 1)
            pool.wait_ge(pconst_ready, 5)
            pool.wait_ge(cst_loaded, 16)
            rsqrt(pair(vec, ISD1), pair(cst, V1), pconst[:, 0:1], 1).then_inc(eps_added, 1)
            pool.wait_ge(eps_added, 2)
            step(pair(vec, SC1), pair(vec, ISD1), pair(cst, G1), ALU.mult)
            step(pair(vec, TM1), pair(vec, SC1), pair(cst, M1), ALU.mult)
            step(pair(vec, SH1), pair(cst, B1), pair(vec, TM1), ALU.subtract)
            half_c = pconst[:, 3:4]
            step(pair(vec, TM1), pair(cst, BIR), pair(cst, BHR), ALU.add)
            step(pair(vec, BR), pair(vec, TM1), half_c.broadcast_to([P, 2]), ALU.mult)
            nc.gpsimd.tensor_tensor(vec[:, BH:BH + 1], cst[:, BHN:BHN + 1], half_c, ALU.mult).then_inc(vec_ready, 1)
            def chunk_rstd(g, k):
                pool.wait_ge(mv_ready, 4 * g + k + 1)
                rsqrt(rstd[:, NB * k:NB * k + NB], mv[:, NB * k:NB * k + NB, 1], pconst[:, 1:2],
                      4 * g + k + 3).then_inc(rstd_ready, 1)

            with pool.Fori(0, NG - 1) as g:
                for k in range(NC):
                    chunk_rstd(g, k)
            for k in range(NC):
                chunk_rstd(NG - 1, k)
                if k == 1:
                    pool.wait_ge(rstd_ready, 4 * (NG - 1) + k + 1)
                    part = slice(NB * k, NB * k + NB)
                    step(shift[:, :], mv[:, part, 0], rstd[:, part], ALU.mult)
                    nc.gpsimd.tensor_tensor(shift[:, :], shift[:, :], pconst[:, 4:5].broadcast_to([P, NB]),
                                            ALU.mult).then_inc(shift_ready, 1)

        @block.vector
        def _(dve):
            steps = [0]

            def step(ins):
                steps[0] += 1
                ins.then_inc(setup_step, 1)
                dve.wait_ge(setup_step, steps[0])

            def v(c):
                return vec[:, c:c + 1]

            def con(c, n=P):
                return cst[0:n, c:c + 1]

            TT, TS, STT = nc.vector.tensor_tensor, nc.vector.tensor_scalar, nc.vector.scalar_tensor_tensor

            def setup_small():
                rows = H[:, :, :].rearrange("p c (b j) -> p (c b) j", b=GB)
                nc.vector.memset(rows[:, :, 0:JP], 0.0)
                nc.vector.memset(rows[:, :, JP + NI:J], 0.0)
                nc.vector.memset(f32(z_hi[:, :]), 0.0)
                nc.vector.memset(f32(ones_r[:, :]), 1.0)
                step(nc.vector.memset(f32(z_lo[:, :]), 0.0))
                dve.wait_ge(whi_ready, 1)
                TT(w_lo[:, 0:NF, :], w_first[:, 3:SM].rearrange("p (a b) -> p a b", b=P), f32(w_hi[:, 0:NF, :]),
                   ALU.subtract).then_inc(small_ready, 1)

            def setup_distance():
                ws = w_first[:, 0:3].rearrange("p (o s) -> p o s", o=1).broadcast_to([P, STACK // 3, 3])
                zh, zl = (t[:, 96:96 + STACK].rearrange("p (q s) -> p q s", s=3) for t in (z_hi, z_lo))
                nc.vector.tensor_copy(zh, ws)
                dve.wait_ge(bias_loaded, 48)
                step(nc.vector.tensor_copy(bmsg_r[:, :], bmsg[:, :]))
                TT(zl, ws, f32(zh), ALU.subtract)
                dve.wait_ge(cst_loaded, 16)
                STT(bmsg_r[:, :], f32(bmsg_r[:, :]), con(KNM, 2), bmsg[:, :], ALU.mult,
                    ALU.add).then_inc(small_ready, 1)

            def setup_bias():
                dve.wait_ge(bse_spread, 1)
                step(nc.vector.tensor_copy(v(BSE), bank[7][:, 0:1]))
                dve.wait_ge(vec_ready, 1)
                STT(v(BL), v(BSE), con(KAL), con(KCL), ALU.mult, ALU.add)
                STT(v(BRR), v(BSE), con(KAR), con(KCR), ALU.mult, ALU.add)
                TS(v(NSC2), v(SC2), -1.0, None, ALU.mult).then_inc(small_ready, 1)

            def setup_sum(i, a, b):
                t = taps[:, :, :].rearrange("p (g k) o -> p g k o", k=4)
                return TT(tapsum[i], t[:, :, a, :], t[:, :, b, :], ALU.add)

            def setup_gates_lo():
                dve.wait_ge(whi_ready, 2)
                TT(w_lo[:, NF:, :], w_rest.rearrange("p (a b) -> p a b", b=P), f32(w_hi[:, NF:, :]),
                   ALU.subtract).then_inc(gatesw_ready, 1)

            lo_sums, hi_sums = (c[:, TAPS:, :].rearrange("p (s g) o -> p s g o", g=TG) for c in (cw_lo, cw_hi))

            def setup_sum_lo(s, n):
                dve.wait_ge(cwhi_ready, n)
                return TT(lo_sums[:, s], tapsum[s], f32(hi_sums[:, s]), ALU.subtract)

            def setup_last_tap_lo(n):
                dve.wait_ge(cwhi_ready, n)
                return TT(cw_lo[:, TAPS - 1:TAPS, :], last_tap[:, :, :], f32(cw_hi[:, TAPS - 1:TAPS, :]),
                          ALU.subtract)

            def setup_taps_lo(f, n):
                dve.wait_ge(cwhi_ready, n)
                dst, src, hi = (t[:, 0:TAPS - 1, :].rearrange("p (g k) o -> p g k o", k=4)[:, :, f]
                                for t in (cw_lo, taps, cw_hi))
                return TT(dst, src, f32(hi), ALU.subtract)

            def split_x(g, k, first):
                dve.wait_ge(xhi_ready, 4 * g + k + 1)
                src = x_first[:, k - 2] if first and k >= 2 else xs[:, k % 2]
                TT(chunk(x_lo, k), src, f32(chunk(x_hi, k)), ALU.subtract).then_inc(x_ready, 1)

            def shifted(a, n, q):
                flat = H[:, :, :].rearrange("p a b -> p (a b)")
                at = a * SL + q * QS + 1
                return flat[:, at:at + n * SL].rearrange("p (a b) -> p a b", a=n)[:, :, 0:QS]

            def early_differences(g, k):
                dve.wait_ge(h_ready, 4 * g + k + 1)
                TT(EF[:, k % 2, 8, :], part(H, 2, k), part(H, 3, k), ALU.subtract)
                TT(EF[:, k % 2, 9, :], part(H, 3, k), shifted(0, 1, k)[:, 0], ALU.subtract).then_inc(d_ready, 1)

            def early_lo(g, k):
                cols = slice(k * QS, (k + 1) * QS)
                dve.wait_ge(vahi_ready, 4 * g + k + 1)
                TT(part(V_lo, H3, k), part(H, 3, k), f32(part(V_hi, H3, k)), ALU.subtract)
                TT(V_lo[:, D2:D3 + 1, cols], EF[:, k % 2, 8:10, :], f32(V_hi[:, D2:D3 + 1, cols]),
                   ALU.subtract).then_inc(va_ready, 1)

            def slots_e_low():
                TT(E_all[:, 0:2], H[:, 0:2, :], H[:, 2:4, :], ALU.subtract)

            def slots_e_high():
                flat = H[:, :, :].rearrange("p a b -> p (a b)")
                TT(E_all[:, 2:4], H[:, 2:4, :], flat[:, 1:2 * SL + 1].rearrange("p (a b) -> p a b", a=2),
                   ALU.subtract).then_inc(slot_diff, 1)

            def slot_f(c, used):
                dve.wait_ge(slot_lo if used else slot_diff, used or 1)
                nxt = E_all[:, c + 1] if c < 3 else ef[:, 1:SL + 1]
                TT(F_one, E_all[:, c], nxt, ALU.subtract).then_inc(slot_diff, 1)

            def slot_low(slot, src, n):
                dve.wait_ge(slot_hi, n)
                TT(V_lo[:, slot, :], src, f32(V_hi[:, slot, :]), ALU.subtract).then_inc(slot_lo, 1)

            def late_differences_e(g, k):
                cols = slice(k * QS, (k + 1) * QS)
                TT(EF[:, k % 2, 0:2, :], H[:, 0:2, cols], H[:, 2:4, cols], ALU.subtract)
                TT(EF[:, k % 2, 2:4, :], H[:, 2:4, cols], shifted(0, 2, k), ALU.subtract).then_inc(e_ready, 1)

            def late_differences_f(g, k):
                dve.wait_ge(e_ready, 4 * g + k - 3)
                first_e = EF[:, k % 2, :, :].rearrange("p a b -> p (a b)")[:, 1:QS + 1]
                TT(EF[:, k % 2, 7, :], EF[:, k % 2, 3, :], first_e, ALU.subtract)
                TT(EF[:, k % 2, 4:7, :], EF[:, k % 2, 0:3, :], EF[:, k % 2, 1:4, :], ALU.subtract).then_inc(ef_ready, 1)

            def late_lo(g, k):
                cols = slice(k * QS, (k + 1) * QS)
                dve.wait_ge(vbhi_ready, 4 * g + k - 3)
                TT(V_lo[:, F0:F3 + 1, cols], EF[:, k % 2, 4:8, :], f32(V_hi[:, F0:F3 + 1, cols]), ALU.subtract)
                TT(V_lo[:, E1:E3 + 1, cols], odd_e(k), f32(V_hi[:, E1:E3 + 1, cols]),
                   ALU.subtract).then_inc(vb_ready, 1)

            def square_rows(g, q):
                dve.wait_ge(affine_ready, 2 * g + q + 1)
                STT(VL[:, q, 0:N], SQ[:, q], con(KSL), VL[:, q, 0:N], ALU.mult, ALU.add)
                STT(VR[:, q, 0:N], SQ[:, q], con(KSR), VR[:, q, 0:N], ALU.mult, ALU.add).then_inc(rows_ready, 1)

            def operands(g, q):
                dve.wait_ge(lrhi_ready, 2 * g + q + 1)
                STT(L[:, q, :], f32(L[:, q, :]), con(KNL), VL[:, q, 0:N], ALU.mult, ALU.add)
                STT(R[:, q, :], f32(R[:, q, :]), con(KNR), VR[:, q, 0:N], ALU.mult, ALU.add).then_inc(lr_ready, 1)

            def mask(g, b):
                if b % 2 == 0:
                    dve.wait_ge(adj_loaded[b // 2 % 2], 32 * g + 16 * (b // 4) + 16)
                dve.wait_ge(exp_ready, 8 * g + b + 1)
                TT(A[:, b % 2, :], A[:, b % 2, :], adj[:, b // 2 % 2, b % 2].rearrange("p m n -> p (m n)"),
                   ALU.mult).then_inc(a_ready, 1)

            def message_sum(g, b):
                dve.wait_ge(msg_half, 8 * g + b + 1)
                t = msg_bank[:, :].rearrange("p (m h d) -> p m h d", m=MB, h=2)
                TT(msg[:, b % 2], t[:, :, 0], msg[:, b % 2], ALU.add).then_inc(msg_summed, 1)

            def sums_lo(g, pair):
                dve.wait_ge(mhi_ready, 4 * g + pair + 1)
                TT(chunk(m_lo, pair), nmp_bank[pair % 2][:, :], f32(chunk(m_hi, pair)),
                   ALU.subtract).then_inc(m_ready, 1)

            def product(g, j, side, first):
                n = 3 * j + 1 + side
                dve.wait_ge(s_ready, 3 * g + j + 1)
                dve.wait_ge(conv2_done, NP * g + n + 1)
                if j == 0 and side == 0 and not first:
                    dve.wait_ge(vb_ready, 4 * g)
                P1 = P1_first if first else P1_later
                dst = grid(P1[:, side, :]) if j == 0 else inner(2 * (j - 1) + side)
                src, shr = conv2_bank[n % 2][:, :], (S_first if first else S_later)[j]
                if not first and j == 0:
                    src, dst = (t.rearrange("p (h n) -> p h n", h=2) for t in (src, P1[:, side, :]))
                else:
                    src, shr = grid(src), grid(shr)
                STT(dst, src, v(NSC2 if side else SC2), shr, ALU.mult, ALU.add).then_inc(prod_used, 1)

            def conv_sum(g, c, first):
                j, side = 1 + c // 2, c % 2
                t, p1 = inner(c), grid((P1_first if first else P1_later)[:, side, :])
                dve.wait_ge(prod_used, 6 * g + 2 * j + side + 1)
                if c < 2:
                    TT(t, p1, t, ALU.add).then_inc(t_step, 1)
                    dve.wait_ge(t_step, 4 * g + 2 * c + 1)
                    TT(t, t, phase(x, c), ALU.add).then_inc(t_ready, 1)
                    TT(p1, p1, phase(x, c + 2), ALU.add).then_inc(t_step, 1)
                else:
                    dve.wait_ge(t_step, 4 * g + 2 * (c - 2) + 2)
                    TT(t, p1, t, ALU.subtract).then_inc(t_ready, 1)

            def conv_lo(g, c):
                dve.wait_ge(chi_ready, 4 * g + c + 1)
                STT(phase(c_lo, c), inner(c), 0.0, f32(phase(c_hi, c)), ALU.max, ALU.subtract).then_inc(c_ready, 1)

            def rows(k):
                return xn[:, NB * k:NB * k + NB, :]

            def residual(g, k):
                dve.wait_ge(turn_done, 4 * g + k + 1)
                dve.wait_ge(xn_loaded[k], 16 * g + 16)
                STT(rows(k), rows(k), 4.0, turn_bank[k % 2][:, :].rearrange("p (a d) -> p a d", a=NB), ALU.mult,
                    ALU.add).then_inc(y_ready, 1)

            def norm_stats(g, k):
                dve.wait_ge(y_ready, 4 * g + k + 1)
                for j in range(NB):
                    last = nc.vector.bn_stats(stats[:, NB * k + j, :], rows(k)[:, j, :])
                last.then_inc(stats_ready, 1)

            def norm_mean(k):
                for j in range(NB * k, NB * k + NB):
                    last = nc.vector.bn_aggr(mv[:, j, :], stats[:, j, :])
                last.then_inc(mv_ready, 1)

            def normalise(g, k):
                dve.wait_ge(rstd_ready, 4 * g + k + 1)
                for j in range(NB):
                    y, n = rows(k)[:, j, :], NB * k + j
                    last = TS(y, y, mv[:, n, 0:1], rstd[:, n:n + 1], ALU.subtract, ALU.mult)
                last.then_inc(out_ready, 1)

            def mix_stage(g, prev):
                def norm(what, *args):
                    if prev is not None:
                        what(*args)

                def stats_done(k):
                    norm(lambda: dve.wait_ge(stats_ready, 4 * prev + k + 1))
                first = prev is None

                def late_differences(k):
                    late_differences_e(g, k)
                    late_differences_f(g, k)
                norm(square_rows, g, 0)
                norm(message_sum, g, 0)
                norm(residual, prev, NC - 1)
                if first:
                    dve.wait_ge(va_ready, NC)
                    slots_e_low()
                    operands(g, 0)
                    setup_sum_lo(1, 3).then_inc(cw_ready, 1)
                    slots_e_high()
                    operands(g, 1)
                    setup_sum_lo(2, 4).then_inc(cw_ready, 1)
                    slot_f(0, 0)
                    mask(g, 0)
                    slot_low(E1, E_all[:, 1], 1)
                    setup_sum_lo(0, 5).then_inc(cw_ready, 1)
                else:
                    square_rows(g, 1)
                    operands(g, 0)
                    late_differences(2)
                    late_differences(3)
                    mask(g, 0)
                    late_lo(g, 2)
                    late_lo(g, 3)
                product(g, 0, 0, first)
                message_sum(g, 1)
                mask(g, 1)
                if first:
                    setup_gates_lo()
                    slot_low(F0, F_one, 2)
                    slot_f(1, 2)
                else:
                    operands(g, 1)
                norm(norm_stats, prev, 0)
                norm(norm_stats, prev, 1)
                product(g, 0, 1, first)
                if first:
                    setup_sum_lo(3, 6).then_inc(sum23_ready, 1)
                message_sum(g, 2)
                stats_done(1)
                mask(g, 2)
                norm(norm_mean, 0)
                norm(norm_mean, 1)
                if first:
                    setup_taps_lo(0, 7).then_inc(cw_ready, 1)
                    slot_low(F1, F_one, 3)
                    setup_taps_lo(1, 7).then_inc(cw_ready, 1)
                sums_lo(g, 0)
                if first:
                    slot_f(2, 3)
                norm(norm_stats, prev, 2)
                norm(norm_stats, prev, 3)
                message_sum(g, 3)
                stats_done(3)
                mask(g, 3)
                norm(norm_mean, 2)
                norm(norm_mean, 3)
                norm(normalise, prev, 0)
                norm(normalise, prev, 1)
                if first:
                    slot_low(E3, E_all[:, 3], 4)
                    slot_low(F2, F_one, 5)
                    slot_f(3, 5)
                product(g, 1, 0, first)
                message_sum(g, 4)
                mask(g, 4)
                for k in range(NC):
                    dve.wait_ge(x_loaded[k], 16 * g + 16)
                conv_sum(g, 0, first)
                norm(normalise, prev, 2)
                sums_lo(g, 1)
                product(g, 1, 1, first)
                message_sum(g, 5)
                mask(g, 5)
                if first:
                    slot_low(F3, F_one, 6)
                    setup_taps_lo(2, 7).then_inc(cw_ready, 1)
                conv_sum(g, 1, first)
                conv_lo(g, 0)
                message_sum(g, 6)
                mask(g, 6)
                norm(normalise, prev, 3)
                if first:
                    setup_taps_lo(3, 7).then_inc(cw_ready, 1)
                sums_lo(g, 2)
                conv_lo(g, 1)
                product(g, 2, 0, first)
                message_sum(g, 7)
                conv_sum(g, 2, first)
                mask(g, 7)
                conv_lo(g, 2)
                product(g, 2, 1, first)
                conv_sum(g, 3, first)
                sums_lo(g, 3)
                conv_lo(g, 3)

            def gru_stage(g, last):
                for k in range(NC):
                    rk, zk, hk = r[:, k % 2, :], z[:, k % 2, :], hn[:, k % 2, :]
                    if not last and k == 0:
                        split_x(g + 1, 0, False)
                    dve.wait_ge(r_ready, 4 * g + k + 1)
                    dve.wait_ge(hn_ready, 4 * g + k + 1)
                    STT(hk, rk, 1.0, hk, ALU.add, ALU.mult).then_inc(gated_ready, 1)
                    if not last and k in (1, 2):
                        late_lo(g + 1, k - 1)
                    dve.wait_ge(gated_ready, 4 * g + k + 1)
                    dve.wait_ge(in_done, 4 * g + k + 1)
                    TT(hk, hk, in_bank[:, :], ALU.add).then_inc(narg_ready, 1)
                    if k >= 1:
                        residual(g, k - 1)
                    if not last:
                        early_differences(g + 1, k)
                    dve.wait_ge(n_ready, 4 * g + k + 1)
                    TT(rk, chunk(x, k), hk, ALU.subtract).then_inc(diff_ready, 1)
                    if not last and k < 2:
                        late_differences_e(g + 1, k)
                    dve.wait_ge(diff_ready, 4 * g + k + 1)
                    dve.wait_ge(z_ready, 4 * g + k + 1)
                    STT(rk, zk, -1.0, rk, ALU.add, ALU.mult).then_inc(f_ready, 1)
                    if last and k >= 1:
                        norm_stats(g, k - 1)
                        dve.wait_ge(stats_ready, 4 * g + k)
                        if k < NC - 1:
                            norm_mean(k - 1)
                        if k == 2:
                            normalise(g, 0)
                    if not last:
                        if k < 2:
                            late_differences_f(g + 1, k)
                        if k < NC - 1:
                            split_x(g + 1, k + 1, False)
                        early_lo(g + 1, k)
                if last:
                    residual(g, NC - 1)
                    norm_mean(NC - 2)
                    norm_stats(g, NC - 1)
                    dve.wait_ge(stats_ready, 4 * g + NC)
                    norm_mean(NC - 1)
                    for k in range(2, NC):
                        normalise(g, k)

            setup_small()
            split_x(0, 0, True)
            split_x(0, 1, True)
            setup_distance()
            split_x(0, 2, True)
            split_x(0, 3, True)
            early_differences(0, 0)
            setup_bias()
            early_differences(0, 1)
            early_lo(0, 0)
            dve.wait_ge(taps_loaded, 32)
            setup_sum(0, 0, 1)
            dve.wait_ge(va_ready, 1)
            early_differences(0, 2)
            early_lo(0, 1)
            dve.wait_ge(va_ready, 2)
            early_differences(0, 3)
            early_lo(0, 2)
            step(setup_sum(3, 2, 3))
            TT(tapsum[4], tapsum[0], tapsum[3], ALU.add).then_inc(tapsum_ready, 1)
            early_lo(0, 3)
            setup_last_tap_lo(1)
            setup_sum_lo(4, 2).then_inc(cw_ready, 1)
            square_rows(0, 0)
            message_sum(0, 0)
            setup_sum(1, 0, 2).then_inc(tapsum_ready, 1)
            setup_sum(2, 1, 3).then_inc(tapsum_ready, 1)
            square_rows(0, 1)
            mix_stage(0, None)
            with dve.Fori(0, NG - 1) as g:
                gru_stage(g, False)
                mix_stage(g + 1, g)
            gru_stage(NG - 1, True)


def constants():
    con = np.zeros((P, KSR - KAL + 1), np.float32)
    selb = np.zeros((3, P), np.float32)
    for q in range(4):
        for row in range(STACK):
            kind, at = row // 3, 32 * q + row
            con[at, KAL - KAL] = kind < 4
            con[at, KCL - KAL] = kind >= 6
            con[at, KAR - KAL] = 2 * (kind < 4)
            con[at, KCR - KAL] = -(kind in (4, 5))
            con[at, KSL - KAL] = kind in (4, 5)
            con[at, KSR - KAL] = -(kind >= 6)
            con[at, KNL - KAL] = -(kind in (2, 3, 5))
            con[at, KNR - KAL] = -(kind in (1, 3, 7))
            selb[row % 3, at] = 1
    con[1, KNM - KAL] = -1
    return con, selb, np.eye(P, dtype=np.float32)


def kernel(**inputs):
    import concourse.bacc as bacc
    from concourse.bass_utils import run_bass_kernel_spmd

    a = {k.replace("L0_gnn_", ""): np.asarray(v) for k, v in inputs.items()}
    x, adj = a["x"], a["adj"]
    xp = x.reshape(B, NI, PH, P).transpose(0, 2, 1, 3).reshape(B, N, P)
    ap = adj.reshape(B, NI, PH, NI, PH).transpose(0, 2, 1, 4, 3).reshape(B, N, N)
    w_ih, w_hh = a["w_ih"], a["w_hh"]
    blocks = ([a["w_se"].T, a["conv1_w"][:, :, 0].T, a["w_msg"].T] +
              [w_hh[i * P:(i + 1) * P].T for i in range(3)] +
              [w_ih[i * P:(i + 1) * P, :P].T for i in range(3)] +
              [w_ih[i * P:(i + 1) * P, P:].T for i in range(3)])
    b_ih, b_hh = a["b_ih"].reshape(3, P), a["b_hh"].reshape(3, P)
    par = [a[f"bn{i}_{what}"] for what in "gbmv" for i in (1, 2)]
    par += [b_ih[0], b_ih[1], b_hh[0], b_hh[1], b_hh[2], b_ih[2]]
    con, selb, idn = constants()
    arrays = {
        "xt": xp.reshape(NG, C, P).transpose(0, 2, 1),
        "xn": xp.reshape(NG, C // P, P, P).transpose(0, 2, 1, 3),
        "adj": ap.transpose(0, 2, 1).reshape(NG, 4, 2, MB, P, N).transpose(0, 1, 4, 2, 3, 5),
        "wsm": np.concatenate(blocks, axis=1),
        "wcv": a["conv2_w"].transpose(1, 2, 0),
        "cst": np.concatenate([np.stack(par, axis=1), con, idn], axis=1),
        "bmsg": np.stack([a["b_msg"], a["b_msg"]]),
        "bse": a["b_se"].reshape(3, 1),
        "selb": selb,
    }
    arrays = {k + "_dram": np.ascontiguousarray(v) for k, v in arrays.items()}
    nc = bacc.Bacc("TRN2", target_bir_lowering=False, num_devices=1)
    drams = [nc.dram_tensor(k, v.shape, F32, kind="ExternalInput").ap() for k, v in arrays.items()]
    out = nc.dram_tensor("out_dram", (NG, P, C // P, P), F32, kind="ExternalOutput").ap()
    build(nc, *drams, out)
    res = run_bass_kernel_spmd(nc, [arrays], core_ids=[0]).results[0]["out_dram"]
    y = res.transpose(0, 2, 1, 3).reshape(B, PH, NI, P).transpose(0, 2, 1, 3).reshape(B, N, P)
    return np.ascontiguousarray(y)
```
